# Optimizing a Trainium2 kernel written in Bass

```python
import numpy as np
import jax
import jax.numpy as jnp

def _softmax(x, axis=-1):
    return jax.nn.softmax(x, axis=axis)

def _gelu(x):
    return jax.nn.gelu(x, approximate=True)

def _silu(x):
    return jax.nn.silu(x)

def _sigmoid(x):
    return jax.nn.sigmoid(x)

def _layernorm(x, axis=-1, eps=1e-05):
    m = jnp.mean(x, axis=axis, keepdims=True)
    v = jnp.var(x, axis=axis, keepdims=True)
    return (x - m) / jnp.sqrt(v + eps)

def _scatter_add(tgt, idx, src, axis=0):
    return tgt.at[idx].add(src)

def _segment_sum(src, seg, n):
    return jax.ops.segment_sum(src, seg, n)
kernel_name = 'mk_seq_postln_d1_jaxref_r8_b64897'

def setup_inputs(seed: int=0):
    np.random.seed(seed)
    _w = jnp.asarray

    def _L0_attn_setup():
        import jax, jax.numpy as jnp
        import numpy as np
        N_EMBD = 128
        N_HEAD = 16
        HORIZON = 64
        HS = N_EMBD // N_HEAD
        BD = max(HS // 4, 16)

        def _windows(t, delta):
            B, nh, T, D = t.shape
            padded = jnp.pad(t, ((0, 0), (0, 0), (delta - 1, 0), (0, 0)))
            idx = jnp.arange(T)[:, None] + jnp.arange(delta)[None, :]
            return padded[:, :, idx]
        key = jax.random.key(seed)
        ks = jax.random.split(key, 12)
        s = 0.02
        B, T = (2, 128)
        return {'x': jax.random.normal(ks[0], (B, T, N_EMBD), jnp.float32), 'W_disp': jax.random.normal(ks[1], (N_EMBD, N_HEAD * BD), jnp.float32) * s, 'W_val': jax.random.normal(ks[2], (N_EMBD, N_EMBD), jnp.float32) * s, 'rel_pos_emb': jax.random.normal(ks[3], (HORIZON, BD), jnp.float32) * s, 'W_strain': jax.random.normal(ks[4], (BD, BD), jnp.float32) * s, 'W_pos': jax.random.normal(ks[5], (BD, BD), jnp.float32) * s, 'W_bond': jax.random.normal(ks[6], (BD, 1), jnp.float32) * s, 'W_dmg': jax.random.normal(ks[7], (BD, BD), jnp.float32) * s, 'b_dmg': jnp.zeros((BD,), jnp.float32), 'W_dmg_out': jax.random.normal(ks[8], (BD, 1), jnp.float32) * s, 'b_dmg_out': jnp.full((1,), -3.0, jnp.float32), 'W_cproj': jax.random.normal(ks[9], (N_EMBD, N_EMBD), jnp.float32) * s}
    _L0_attn_in = _L0_attn_setup()

    def _L0_ffn_setup():
        import jax, jax.numpy as jnp
        import numpy as np
        D_IN, D_HID = (128, 512)

        def _ternary(key, shape):
            return jax.random.randint(key, shape, -1, 2).astype(jnp.float32)

        def _tlin(x, w, s):
            return jnp.einsum('bsi,oi->bso', x, w) * s
        key = jax.random.key(seed)
        ks = jax.random.split(key, 12)
        inv = lambda fan: 1.0 / np.sqrt(fan).astype(np.float32)
        return {'x': jax.random.normal(ks[0], (4, 256, D_IN), dtype=jnp.float32), 'w1_w': _ternary(ks[1], (D_HID, D_IN)), 'w1_s': jax.random.uniform(ks[2], (D_HID,), dtype=jnp.float32) * inv(D_IN), 'w2_w': _ternary(ks[3], (D_HID, D_IN)), 'w2_s': jax.random.uniform(ks[4], (D_HID,), dtype=jnp.float32) * inv(D_IN), 'h1_w': _ternary(ks[5], (D_HID, D_HID)), 'h1_s': jax.random.uniform(ks[6], (D_HID,), dtype=jnp.float32) * inv(D_HID), 'h2_w': _ternary(ks[7], (D_HID, D_HID)), 'h2_s': jax.random.uniform(ks[8], (D_HID,), dtype=jnp.float32) * inv(D_HID), 'w3_w': _ternary(ks[9], (D_IN, D_HID)), 'w3_s': jax.random.uniform(ks[10], (D_IN,), dtype=jnp.float32) * inv(D_HID)}
    _L0_ffn_in = _L0_ffn_setup()
    _d = {'L0_attn_x': _L0_attn_in['x'], 'L0_attn_W_disp': _L0_attn_in['W_disp'], 'L0_attn_W_val': _L0_attn_in['W_val'], 'L0_attn_rel_pos_emb': _L0_attn_in['rel_pos_emb'], 'L0_attn_W_strain': _L0_attn_in['W_strain'], 'L0_attn_W_pos': _L0_attn_in['W_pos'], 'L0_attn_W_bond': _L0_attn_in['W_bond'], 'L0_attn_W_dmg': _L0_attn_in['W_dmg'], 'L0_attn_b_dmg': _L0_attn_in['b_dmg'], 'L0_attn_W_dmg_out': _L0_attn_in['W_dmg_out'], 'L0_attn_b_dmg_out': _L0_attn_in['b_dmg_out'], 'L0_attn_W_cproj': _L0_attn_in['W_cproj'], 'L0_ffn_w1_w': _L0_ffn_in['w1_w'], 'L0_ffn_w1_s': _L0_ffn_in['w1_s'], 'L0_ffn_w2_w': _L0_ffn_in['w2_w'], 'L0_ffn_w2_s': _L0_ffn_in['w2_s'], 'L0_ffn_h1_w': _L0_ffn_in['h1_w'], 'L0_ffn_h1_s': _L0_ffn_in['h1_s'], 'L0_ffn_h2_w': _L0_ffn_in['h2_w'], 'L0_ffn_h2_s': _L0_ffn_in['h2_s'], 'L0_ffn_w3_w': _L0_ffn_in['w3_w'], 'L0_ffn_w3_s': _L0_ffn_in['w3_s']}
    _x0 = _d['L0_attn_x']
    _d['L0_attn_x'] = jax.random.normal(jax.random.fold_in(jax.random.key(seed), 1), (16, 512, 128), dtype=_x0.dtype)
    del _x0
    return _d

def reference(L0_attn_x, L0_attn_W_disp, L0_attn_W_val, L0_attn_rel_pos_emb, L0_attn_W_strain, L0_attn_W_pos, L0_attn_W_bond, L0_attn_W_dmg, L0_attn_b_dmg, L0_attn_W_dmg_out, L0_attn_b_dmg_out, L0_attn_W_cproj, L0_ffn_w1_w, L0_ffn_w1_s, L0_ffn_w2_w, L0_ffn_w2_s, L0_ffn_h1_w, L0_ffn_h1_s, L0_ffn_h2_w, L0_ffn_h2_s, L0_ffn_w3_w, L0_ffn_w3_s):

    def _L0_attn_ref(x, W_disp, W_val, rel_pos_emb, W_strain, W_pos, W_bond, W_dmg, b_dmg, W_dmg_out, b_dmg_out, W_cproj):
        import jax, jax.numpy as jnp
        import numpy as np
        N_EMBD = 128
        N_HEAD = 16
        HORIZON = 64
        HS = N_EMBD // N_HEAD
        BD = max(HS // 4, 16)

        def _windows(t, delta):
            B, nh, T, D = t.shape
            padded = jnp.pad(t, ((0, 0), (0, 0), (delta - 1, 0), (0, 0)))
            idx = jnp.arange(T)[:, None] + jnp.arange(delta)[None, :]
            return padded[:, :, idx]
        B, T, C = x.shape
        nh, bd, hs = (N_HEAD, BD, HS)
        delta = min(HORIZON, T)
        disp = (x @ W_disp).reshape(B, T, nh, bd).transpose(0, 2, 1, 3)
        val = (x @ W_val).reshape(B, T, nh, hs).transpose(0, 2, 1, 3)
        disp_win = _windows(disp, delta)
        val_win = _windows(val, delta)
        cmask = jnp.arange(T)[:, None] - delta + 1 + jnp.arange(delta)[None, :] >= 0
        strain = disp_win - disp[:, :, :, None, :]
        rel_emb = rel_pos_emb[:delta]
        bond_act = jax.nn.gelu(strain @ W_strain + rel_emb @ W_pos, approximate=False)
        bond_logits = (bond_act @ W_bond)[..., 0]
        damage_act = jax.nn.gelu(strain @ W_dmg + b_dmg, approximate=False)
        damage = jax.nn.sigmoid((damage_act @ W_dmg_out)[..., 0] + b_dmg_out[0])
        logits = bond_logits - 10.0 * damage
        logits = jnp.where(cmask[None, None], logits, -jnp.inf)
        weights = jax.nn.softmax(logits, axis=-1)
        out = jnp.einsum('bntd,bntde->bnte', weights, val_win)
        out = out.transpose(0, 2, 1, 3).reshape(B, T, C)
        return out @ W_cproj

    def _L0_ffn_ref(x, w1_w, w1_s, w2_w, w2_s, h1_w, h1_s, h2_w, h2_s, w3_w, w3_s):
        import jax, jax.numpy as jnp
        import numpy as np
        D_IN, D_HID = (128, 512)

        def _ternary(key, shape):
            return jax.random.randint(key, shape, -1, 2).astype(jnp.float32)

        def _tlin(x, w, s):
            return jnp.einsum('bsi,oi->bso', x, w) * s
        h = jax.nn.silu(_tlin(x, w1_w, w1_s)) * _tlin(x, w2_w, w2_s)
        h = jax.nn.gelu(_tlin(h, h1_w, h1_s), approximate=False)
        h = jax.nn.gelu(_tlin(h, h2_w, h2_s), approximate=False)
        return _tlin(h, w3_w, w3_s)
    x = L0_attn_x
    x = _layernorm(x + _L0_attn_ref(x, L0_attn_W_disp, L0_attn_W_val, L0_attn_rel_pos_emb, L0_attn_W_strain, L0_attn_W_pos, L0_attn_W_bond, L0_attn_W_dmg, L0_attn_b_dmg, L0_attn_W_dmg_out, L0_attn_b_dmg_out, L0_attn_W_cproj), axis=-1)
    x = _layernorm(x + _L0_ffn_ref(x, L0_ffn_w1_w, L0_ffn_w1_s, L0_ffn_w2_w, L0_ffn_w2_s, L0_ffn_h1_w, L0_ffn_h1_s, L0_ffn_h2_w, L0_ffn_h2_s, L0_ffn_w3_w, L0_ffn_w3_s), axis=-1)
    return x

_drawn_inputs = setup_inputs


def setup_inputs(seed=0):
    import zlib

    import numpy as np

    out = dict(_drawn_inputs(seed))
    spreads = {'L0_attn_b_dmg': (0.0, 0.8)}
    factors = {'L0_attn_W_disp': 8.0,
     'L0_attn_W_val': 7.226,
     'L0_attn_rel_pos_emb': 8.0,
     'L0_attn_W_strain': 8.0,
     'L0_attn_W_pos': 8.0,
     'L0_attn_W_bond': 8.0,
     'L0_attn_W_dmg': 8.0,
     'L0_attn_W_dmg_out': 8.0,
     'L0_attn_W_cproj': 7.244,
     'L0_ffn_w1_w': 8.0,
     'L0_ffn_w1_s': 8.0,
     'L0_ffn_w2_w': 8.0,
     'L0_ffn_w2_s': 8.0,
     'L0_ffn_h1_w': 8.0,
     'L0_ffn_h1_s': 8.0,
     'L0_ffn_h2_w': 8.0,
     'L0_ffn_h2_s': 8.0,
     'L0_ffn_w3_w': 8.0,
     'L0_ffn_w3_s': 8.0}
    for name, (base, spread) in spreads.items():
        noise = np.random.default_rng([zlib.crc32(name.encode()), seed]).standard_normal(out[name].shape)
        drawn = base * np.exp(spread * noise) if base else spread * noise
        out[name] = jnp.asarray(drawn.astype(out[name].dtype))
    for name, factor in factors.items():
        out[name] = (out[name] * factor).astype(out[name].dtype)
    return out
```

```python
from contextlib import ExitStack

import concourse.bass as bass
from concourse import mybir

F32 = mybir.dt.float32
ALU = mybir.AluOpType
ACT = mybir.ActivationFunctionType
AX = mybir.AxisListType

P = 128
H = 16
HH = 8
BD = 16
HS = 8
LAGS = 64
NG = 8
LPAD = 8
LN_EPS = 1e-5
MASKED = -1e30
NCH = 4 * NG
NSLOT = NCH + 2
LAG_B = 2
NB = 512 // 64
ZROW = 128
BOND, DMG = 0, 1


def act_order():
    order = []
    for k in range(NSLOT):
        if k < NCH:
            order.append((DMG, k))
        if k >= LAG_B:
            order.append((BOND, k - LAG_B))
    return order


ACT_ORDER = act_order()
ACT_INDEX = {c: n for n, c in enumerate(ACT_ORDER)}
NACT = len(ACT_ORDER)
DVE_CHUNKS = [c for c in ACT_ORDER if c[0] == BOND or c[1] % 4 == 0]
POOL_CHUNKS = [c for c in ACT_ORDER if c[0] == DMG and c[1] % 4 != 0]
NDVE, NPOOL = len(DVE_CHUNKS), len(POOL_CHUNKS)
ZV_RING, ZP_RING, G_RING = 2, 2, 4

ITEMS = [
    ("gate0", 0, "mlp"), ("up0", 1, "mlp"), ("maxT", 2, "att"), ("gate1", 0, "mlp"), ("up1", 1, "mlp"),
    ("maxTT", 2, "att"), ("gate2", 0, "mlp"), ("up2", 1, "mlp"), ("maxB", 2, "att"), ("gate3", 0, "mlp"),
    ("up3", 1, "mlp"), ("h1_0", 0, "mlp"), ("ev0a", 2, "att"), ("h1_1", 1, "mlp"), ("ev0b", 2, "att"),
    ("ev1a", 2, "att"), ("h1_2", 0, "mlp"), ("ev1b", 2, "att"), ("ev2a", 2, "att"), ("h1_3", 1, "mlp"),
    ("ev2b", 2, "att"), ("ev3a", 2, "att"), ("h2_0", 0, "mlp"), ("ev3b", 2, "att"), ("val0", 1, "att"),
    ("h2_1", 1, "mlp"), ("heads0", 2, "att"), ("val1", 0, "att"), ("h2_2", 0, "mlp"), ("h2_3", 1, "mlp"),
    ("val2", 0, "att"), ("mlpout", 0, "mlp"), ("heads1", 2, "att"), ("val3", 1, "att"), ("cproj", 1, "att"),
    ("yT", 0, "att"),
]
BANK = {name: bank for name, bank, _ in ITEMS}
COUNTED_BY_BLOCKS = ("heads0", "heads1")


def bank_use(it, att, mlp, name, skip=()):
    w = BANK[name]
    here = 0
    for other, b, stage in ITEMS:
        if other == name:
            break
        if b == w and other not in skip and (att if stage == "att" else mlp):
            here += 1
    if isinstance(it, int) and it < 2:
        return here
    uses = {s: sum(1 for o, b, st in ITEMS if b == w and st == s and o not in skip) for s in ("att", "mlp")}
    return uses["att"] * (it - 1) + uses["mlp"] * (it - 2) + here


def block_kernel(nc, xT, x, W_dispT, W_val, relT, W_strain, W_pos, W_bond, W_dmg, b_dmg, W_dmg_out, b_dmg_out,
                 W_cproj, w1T, w1_s, w2T, w2_s, h1T, h1_s, h2T, h2_s, w3T, w3_s, out):
    B, T, C = x.shape
    DH = w1T.shape[1]
    KB = DH // P
    TT = T // P
    assert C == P and T == 512 and H * HS == C

    ZH = (T + LAGS) * ZROW
    scratch = nc.dram_tensor("band_scratch", (H * ZH,), F32)

    ctx = ExitStack()
    with ctx:
        def sb(name, shape):
            return ctx.enter_context(nc.sbuf_tensor(name, shape, F32))

        def pb(name):
            return ctx.enter_context(nc.psum_tensor(name, [P, 512], F32))

        def sem(name):
            return ctx.enter_context(nc.semaphore(name))

        zv = sb("zv", [P, ZV_RING, 2048])
        zp = sb("zp", [P, ZP_RING, 2048])
        gl = sb("gl", [P, G_RING, 2048])
        LFLAT = NG * T + LAGS
        logit = [sb(f"logit{i}", [P, LFLAT]) for i in range(2)]
        esh = sb("esh", [P, 2, NG, P])
        ev = sb("ev", [P, 2, H, LAGS])
        band = sb("band", [P, 2, H, 64])
        AW = LPAD + T
        pair = [sb(f"pair{i}", [P, 2, 2, AW]) for i in range(2)]
        w1t = sb("w1t", [P, DH])
        w2t = sb("w2t", [P, DH])
        h1t = sb("h1t", [P, KB, DH])
        h2t = sb("h2t", [P, KB, DH])
        w3t = sb("w3t", [P, KB, P])
        wpair = sb("wpair", [P, 4, P])
        wval = sb("wval", [P, P])
        wcp = sb("wcp", [P, P])
        ident = sb("ident", [P, P])
        selm = sb("selm", [H, P])
        ones = sb("ones", [P, 4, 32])
        ctr = sb("ctr", [P, 2, 4, 32])
        maskc = sb("maskc", [P, NG, LAGS])
        w3sb = sb("w3sb", [P, P])
        xTp = sb("xTp", [P, T])
        xTv = sb("xTv", [P, LAGS + T + LAGS])
        hid1 = sb("hid1", [P, KB, T])
        hid2 = sb("hid2", [P, KB, T])
        th = sb("th", [P, T])
        yT = sb("yT", [P, T])
        y = sb("y", [P, TT, C])
        res = sb("res", [P, TT, C])
        res2 = sb("res2", [P, TT, C])
        t1 = sb("t1", [P, T])
        t2 = sb("t2", [P, T])
        vpad = sb("vpad", [P, 2, 4, 4, 32])
        max2 = sb("max2", [P, TT * H])
        st = sb("st", [P, TT, 6])
        mv = sb("mv", [P, TT, 2])
        ve = sb("ve", [P, TT])
        rstd = sb("rstd", [P, TT])
        st2 = sb("st2", [P, TT, 6])
        mv2 = sb("mv2", [P, TT, 2])
        ve2 = sb("ve2", [P, TT])
        rstd2 = sb("rstd2", [P, TT])
        mhalf = sb("mhalf", [P, TT])
        mark_ = sb("mark_", [P, 2])
        epst = sb("epst", [P, TT])
        relR = sb("relR", [P, LAGS])
        bcol = sb("bcol", [P, 1])
        boraw = sb("boraw", [P, 1])
        s1 = sb("s1", [P, KB])
        s2 = sb("s2", [P, KB])
        s1h = sb("s1h", [P, KB])
        s12 = sb("s12", [P, KB])
        sh1 = sb("sh1", [P, KB])
        sh2 = sb("sh2", [P, KB])
        m8 = sb("m8", [P, HH])
        cols = sb("cols", [P, 35])

        PA = [pb("PA0"), pb("PA1")]
        PD = pb("PD")
        LB = pb("LB")
        LD = pb("LD")
        W = [pb(f"W{i}") for i in range(3)]

        setup_in = sem("setup_in")
        pool_const = sem("pool_const")
        dve_const = sem("dve_const")
        pe_const = sem("pe_const")
        scratch_zero = sem("scratch_zero")
        xp_in = sem("xp_in")
        xv_in = sem("xv_in")
        xr_in = sem("xr_in")
        proj_ready = sem("proj_ready")
        proj_copied = sem("proj_copied")
        zv_ready = sem("zv_ready")
        zp_ready = sem("zp_ready")
        g_ready = sem("g_ready")
        g_used = sem("g_used")
        tanh_done = sem("tanh_done")
        logit_done = sem("logit_done")
        masked = sem("masked")
        gmax_ready = sem("gmax_ready")
        exp_done = sem("exp_done")
        shifted = [sem(f"shifted{i}") for i in range(2)]
        z_written = [sem(f"z_written{i}") for i in range(TT)]
        band_in = [sem(f"band_in{i}") for i in range(2)]
        band_used = sem("band_used")
        stat_done = sem("stat_done")
        var_ready = sem("var_ready")
        rs_step = sem("rs_step")
        rstd_ready = sem("rstd_ready")
        y_ready = sem("y_ready")
        tanh_gate = sem("tanh_gate")
        res2_ready = sem("res2_ready")
        stat2_done = sem("stat2_done")
        var2_ready = sem("var2_ready")
        rs2_step = sem("rs2_step")
        rstd2_ready = sem("rstd2_ready")
        out_ready = sem("out_ready")
        out_done = sem("out_done")
        recip_done = sem("recip_done")
        vpad_even = sem("vpad_even")
        w_ready = [sem(f"w_ready{i}") for i in range(3)]
        w_free = [sem(f"w_free{i}") for i in range(3)]

        block = ctx.enter_context(nc.Block())

        def iterations(eng, body):
            body(0, 0, True, False, False, True)
            body(1, 1, True, True, False, True)
            body(2, 0, True, True, True, True)
            with eng.Fori(0, (B - 4) // 2) as i:
                body(2 * i + 3, 1, True, True, True, True)
                body(2 * i + 4, 0, True, True, True, True)
            body(B - 1, 1, True, True, True, False)
            body(B, 0, False, True, True, False)
            body(B + 1, 1, False, False, True, False)

        def wait(eng, s, value):
            if not (isinstance(value, int) and value <= 0):
                eng.wait_ge(s, value)

        def chunk_parts(c):
            g, half, par = c // 4, (c // 2) % 2, c % 2
            return g, half, par, 8 * g, T - 8 * g

        def shifted_rows(tile, kind, half, par, n):
            full = tile[:, kind, half, :]
            start = full.offset + LPAD - par - 6
            return bass.AP(tile, start, [list(full.ap[0]), [2, 4], [1, n]])

        wvec = gl[0:16, 0, 0:35]
        wposr = gl[0:16, 0, 64:80]
        wposrep = gl[0:16, 0, 128:256]
        relt = gl[0:16, 0, 256:320]
        rep = gl[0:16, 0, 384:512]
        wdt = gl[:, 1, 0:256].rearrange("p (a c) -> p a c", a=2)
        bdg = gl[:, 2, 0:256].rearrange("p (f c) -> p f c", f=2)
        big = gl[:, 3, 0:512].rearrange("p (g t) -> p g t", g=NG)

        @block.sync
        def _(sp):
            def load(dst, src):
                sp.dma_start(dst, src).then_inc(setup_in, 16)

            col = lambda v: v.rearrange("(a b) -> a b", b=1)
            load(xTp[:, :], xT[:, 0:T])
            load(wvec[:, 0:1], W_bond)
            load(wvec[:, 1:2], W_dmg_out)
            load(wvec[:, 2:3], col(b_dmg))
            load(wvec[:, 3:19], W_strain)
            load(wvec[:, 19:35], W_dmg)
            load(wposr[:, :], W_pos)
            load(relt[:, :], relT)
            load(wdt, W_dispT.rearrange("(a p) c -> p a c", p=P))
            load(boraw[:, :], col(b_dmg_out).partition_broadcast(P).rearrange("p a b -> p (a b)"))
            load(wval[:, :], W_val)
            load(wcp[:, :], W_cproj)
            load(w1t[:, :], w1T)
            load(w2t[:, :], w2T)
            load(h1t[:, :, :], h1T.rearrange("(k p) o -> p k o", p=P))
            load(h2t[:, :, :], h2T.rearrange("(k p) o -> p k o", p=P))
            load(w3t[:, :, :], w3T.rearrange("(k p) o -> p k o", p=P))
            for dst, src in ((s1, w1_s), (s2, w2_s), (sh1, h1_s), (sh2, h2_s)):
                load(dst[:, :], src)
            load(w3sb[:, :], w3_s.partition_broadcast(P))
            sp.wait_ge(dve_const, DVE_ZERO)
            per = H * ZH // P
            zero = scratch[:].rearrange("(p n) -> p n", p=P)
            for q in range(4):
                sp.dma_start(zero[:, q * per // 4:(q + 1) * per // 4],
                             logit[0][:, 0:per // 4]).then_inc(scratch_zero, 16)

            def shift(v, pp, tt):
                if tt == 0:
                    sp.wait_ge(exp_done, v["batch"])
                if tt >= 2:
                    sp.wait_ge(w_ready[2], v["transposed"][tt - 2])
                src = logit[pp][:, :]
                for u8 in range(8):
                    rows = src[16 * u8:16 * u8 + 16, :]
                    view = bass.AP(logit[pp], rows.offset + u8 + P * tt, [list(rows.ap[0]), [T + 8, NG], [1, P]])
                    sp.dma_start(esh[16 * u8:16 * u8 + 16, tt % 2, :, :], view).then_inc(shifted[tt % 2], 16)

            def scratch_write(v, tt):
                sp.wait_ge(w_free[2], v["evicted"][tt])
                dst = bass.AP(scratch, (LAGS + P * tt) * ZROW, [[ZROW, P], [ZH, H], [1, LAGS]])
                sp.dma_start(dst, ev[:, tt % 2, :, :]).then_inc(z_written[tt], 16)

            def band_read(v, k):
                if k >= 2:
                    sp.wait_ge(band_used, v["block"][k])
                for tt in range(max(0, (k - 1) // 2), k // 2 + 1):
                    sp.wait_ge(z_written[tt], v["stored"])
                src = bass.AP(scratch, (LAGS + 64 * k - 63) * (ZROW - 1) + LAGS + 64 * k,
                              [[ZROW - 1, P], [ZH, H], [1, 64]])
                sp.dma_start(band[:, k % 2, :, :], src).then_inc(band_in[k % 2], 16)

            def x_rows(src, b):
                if isinstance(b, int):
                    return src[b:b + 1, :, :].rearrange("b (a p) c -> p (b a) c", p=P)
                return src[bass.ds(b, 1), :, :].rearrange("b (a p) c -> p (b a) c", p=P)

            def x_cols(col):
                return xT[:, bass.ds(col, T)]

            def body(it, par, pair_, att, mlp, nxt):
                pb_, pp = it - 1, 1 - par
                use = lambda name: bank_use(it, att, mlp, name)
                use_ready = lambda name: bank_use(it, att, mlp, name, COUNTED_BY_BLOCKS)

                def fixed(value):
                    return value if isinstance(value, int) else sp.snap(value)

                v = {}
                if nxt:
                    v["made"] = fixed(4 * (it + 1))
                    next_cols = fixed((it + 1) * T)
                if att:
                    v["batch"] = fixed(pb_ + 1)
                    v["normed"] = fixed(4 * pb_)
                    v["stored"] = fixed(16 * (pb_ + 1))
                    v["evicted"] = [fixed(use(f"ev{t}b") + 1) for t in range(TT)]
                    v["transposed"] = [fixed(use_ready(f"ev{t}b") + 1) for t in range(2)]
                    v["block"] = [fixed(NB * pb_ + k - 1) for k in range(NB)]
                    this_cols, this_row = fixed(pb_ * T), fixed(pb_)
                if mlp:
                    v["normed2"] = fixed(4 * (it - 1))
                    out_row = fixed(it - 2)
                if nxt:
                    sp.wait_ge(proj_ready, v["made"])
                    sp.dma_start(xTp[:, :], x_cols(next_cols)).then_inc(xp_in, 16)
                if att:
                    wait(sp, y_ready, v["normed"])
                    if isinstance(it, int) and it == 1:
                        sp.wait_ge(dve_const, DVE_ALL)
                    sp.dma_start(xTv[:, LAGS:LAGS + T], x_cols(this_cols)).then_inc(xv_in, 16)
                    sp.dma_start(res[:, :, :], x_rows(x, this_row)).then_inc(xr_in, 16)
                    if isinstance(it, int) and it == 1:
                        sp.wait_ge(scratch_zero, 64)
                    shift(v, pp, 0)
                    shift(v, pp, 1)
                    scratch_write(v, 0)
                    shift(v, pp, 2)
                    scratch_write(v, 1)
                    shift(v, pp, 3)
                    band_read(v, 0)
                    band_read(v, 1)
                    scratch_write(v, 2)
                    scratch_write(v, 3)
                    for k in range(2, NB):
                        band_read(v, k)
                if mlp:
                    sp.wait_ge(out_ready, v["normed2"])
                    sp.dma_start(x_rows(out, out_row), res2[:, :, :]).then_inc(out_done, 16)

            iterations(sp, body)
            sp.wait_ge(out_done, 16 * B)

        @block.gpsimd
        def _(pool):
            step = [0]

            def link(ins):
                step[0] += 1
                ins.then_inc(pool_const, 1)
                pool.wait_ge(pool_const, step[0])

            link(pool.memset(ident[:, :], 0.0))
            link(pool.affine_select(out=ident[:, :], in_=ident[:, :], compare_op=ALU.not_equal, fill=1.0, base=0,
                                    pattern=[[-1, P]], channel_multiplier=1))
            link(pool.memset(rep, 0.0))
            link(pool.affine_select(out=rep.rearrange("d (h o) -> d h o", h=HH), in_=rep.rearrange("d (h o) -> d h o", h=HH),
                                    compare_op=ALU.not_equal, fill=1.0, base=0, pattern=[[0, HH], [-1, BD]],
                                    channel_multiplier=1))
            link(pool.memset(selm[:, :], 0.0))
            sv = selm[:, :].rearrange("h (l g) -> h l g", l=8)
            link(pool.affine_select(out=sv, in_=sv, compare_op=ALU.not_equal, fill=1.0, base=0,
                                    pattern=[[0, 8], [-1, H]], channel_multiplier=1))
            link(pool.memset(m8[:, :], 1.0))
            link(pool.affine_select(out=m8[:, :], in_=m8[:, :], compare_op=ALU.is_ge, fill=0.0, base=0,
                                    pattern=[[-BD, HH]], channel_multiplier=1))
            link(pool.affine_select(out=m8[:, :], in_=m8[:, :], compare_op=ALU.is_ge, fill=0.0, base=BD - 1,
                                    pattern=[[BD, HH]], channel_multiplier=-1))
            link(pool.memset(big, 3e38))
            link(pool.affine_select(out=maskc[:, :, :], in_=big, compare_op=ALU.is_ge, fill=MASKED, base=15,
                                    pattern=[[-128, NG], [16, LAGS]], channel_multiplier=-1))
            link(pool.memset(mhalf[:, :], -0.5))
            link(pool.memset(epst[:, :], LN_EPS))
            assert step[0] == POOL_CONSTS

            def body(it, par, pair_, att, mlp, nxt):
                for k in range(NSLOT):
                    if pair_ and (DMG, k) in POOL_CHUNKS:
                        n = POOL_CHUNKS.index((DMG, k))
                        g, half, pr, t0, w = chunk_parts(k)
                        if n == 0:
                            pool.wait_ge(proj_copied, 4 * it + 2)
                        old = POOL_CHUNKS[(n - ZP_RING) % NPOOL]
                        wait(pool, g_ready, NACT * (it if n >= ZP_RING else it - 1) + ACT_INDEX[old] + 1)
                        dt_ = pair[par][:, DMG, half, LPAD + t0:LPAD + T]
                        o = zp[:, n % ZP_RING, 0:4 * w].rearrange("p (i t) -> p i t", i=4)
                        pool.tensor_tensor(o, shifted_rows(pair[par], DMG, half, pr, w),
                                           dt_.unsqueeze(1).to_broadcast([P, 4, w]), ALU.subtract).then_inc(zp_ready, 1)
                    if att and k == 33:
                        pool.wait_ge(var_ready, 4 * it)
                        pool.tensor_tensor(ve[:, :], mv[:, :, 1], epst[:, :], ALU.add).then_inc(rs_step, 1)
                        pool.wait_ge(rs_step, it)
                        pool.tensor_tensor(rstd[:, :], ve[:, :], mhalf[:, :], ALU.pow).then_inc(rstd_ready, 1)
                    if mlp and k == 31:
                        pool.wait_ge(var2_ready, 4 * (it - 1))
                        pool.tensor_tensor(ve2[:, :], mv2[:, :, 1], epst[:, :], ALU.add).then_inc(rs2_step, 1)
                        pool.wait_ge(rs2_step, it - 1)
                        pool.tensor_tensor(rstd2[:, :], ve2[:, :], mhalf[:, :], ALU.pow).then_inc(rstd2_ready, 1)

            iterations(pool, body)

        @block.vector
        def _(dve):
            step = [0]

            def mark(ins):
                step[0] += 1
                ins.then_inc(dve_const, 1)

            mark(dve.memset(logit[0][:, :], 0.0))
            mark(dve.memset(logit[1][:, :], 0.0))
            assert step[0] == DVE_ZERO
            mark(dve.memset(xTv[:, :], 0.0))
            mark(dve.memset(vpad[:, :, :, :, :], 0.0))
            mark(dve.memset(ones[:, :, :], 0.0))
            mark(dve.memset(ctr[:, :, :, :], 0.0))
            for q in range(2):
                mark(dve.memset(pair[q][:, :, :, 0:LPAD], 0.0))
            dve.wait_ge(dve_const, step[0])
            for h in range(4):
                mark(dve.memset(ones[:, h, HS * h:HS * h + HS], 1.0))
            dve.wait_ge(setup_in, SETUP_DMAS * 16)
            mark(dve.tensor_copy(wposrep.rearrange("d (h o) -> d h o", h=HH),
                                 wposr.unsqueeze(1).to_broadcast([16, HH, BD])))
            mark(dve.tensor_scalar(bcol[:, :], boraw[:, :], 0.5, None, ALU.mult))
            mark(dve.tensor_scalar(s1h[:, :], s1[:, :], 0.5, None, ALU.mult))
            dve.wait_ge(dve_const, step[0])
            mark(dve.tensor_tensor(s12[:, :], s1h[:, :], s2[:, :], ALU.mult))
            assert step[0] == DVE_A
            dve.wait_ge(pe_const, 1)
            dve.tensor_copy(cols[:, :], LB[:, 0:35]).then_inc(dve_const, 1)
            dve.wait_ge(dve_const, DVE_A + 1)
            dve.wait_ge(pool_const, POOL_CONSTS)
            for f in range(2):
                dve.tensor_tensor(bdg[:, f, :].rearrange("p (h o) -> p h o", h=HH),
                                  m8[:, :].unsqueeze(2).to_broadcast([P, HH, BD]),
                                  cols[:, 3 + BD * f:3 + BD * f + BD].unsqueeze(1).to_broadcast([P, HH, BD]),
                                  ALU.mult).then_inc(dve_const, 1)
            for f in range(2):
                for v in range(4):
                    dve.tensor_scalar(ctr[:, f, v, 8 * v:8 * v + 8], m8[:, :], cols[:, f:f + 1], None,
                                      ALU.mult).then_inc(dve_const, 1)
            dve.wait_ge(pe_const, 2)
            dve.tensor_copy(relR[:, :], LB[:, 64:64 + LAGS]).then_inc(dve_const, 1)
            dve.wait_ge(pe_const, 3)
            dve.tensor_copy(wpair[:, :, :], LD[:, :]).then_inc(dve_const, 1)
            dve.wait_ge(dve_const, DVE_ALL)

            def body(it, par, pair_, att, mlp, nxt):
                pb_, pp, mb = it - 1, 1 - par, it - 2
                use = lambda name: bank_use(it, att, mlp, name)
                use_ready = lambda name: bank_use(it, att, mlp, name, COUNTED_BY_BLOCKS)

                def ready(name):
                    dve.wait_ge(w_ready[BANK[name]], use_ready(name) + 1)

                def differences(kind, c):
                    n = DVE_CHUNKS.index((kind, c))
                    g, half, pr, t0, w = chunk_parts(c)
                    dve.wait_ge(proj_copied, 4 * it + (2 if kind == DMG else 3 + half))
                    old = DVE_CHUNKS[(n - ZV_RING) % NDVE]
                    wait(dve, g_ready, NACT * (it if n >= ZV_RING else it - 1) + ACT_INDEX[old] + 1)
                    z = zv[:, n % ZV_RING, 0:4 * w].rearrange("p (i t) -> p i t", i=4)
                    if kind == DMG:
                        dve.tensor_tensor(z, shifted_rows(pair[par], DMG, half, pr, w),
                                          PD[:, t0:T].unsqueeze(1).to_broadcast([P, 4, w]),
                                          ALU.subtract).then_inc(zv_ready, 1)
                        return
                    rows = shifted_rows(pair[par], BOND, half, pr, w)
                    for i in range(4):
                        lag = 8 * g + 2 * (3 - i) + pr
                        ins = dve.scalar_tensor_tensor(out=z[:, i, :], in0=rows[:, i, :],
                                                       scalar=relR[:, 63 - lag:64 - lag], in1=PA[half][:, t0:T],
                                                       op0=ALU.add, op1=ALU.subtract)
                    ins.then_inc(zv_ready, 1)

                def combine(it, par, g):
                    if isinstance(it, int) and it == 0 and g == 0:
                        dve.wait_ge(scratch_zero, 64)
                    if g == 0:
                        wait(dve, shifted[0], 256 * (it - 1))
                        wait(dve, shifted[1], 256 * (it - 1))
                    dve.wait_ge(tanh_done, NG * it + g + 1)
                    dve.wait_ge(g_used, NACT * it + ACT_INDEX[(BOND, 4 * g + 3)] + 1)
                    dve.scalar_tensor_tensor(out=logit[par][:, T * g + 8 * g:T * g + T], in0=th[:, 8 * g:T], scalar=-5.0,
                                             in1=LB[:, 8 * g:T], op0=ALU.mult, op1=ALU.add).then_inc(logit_done, 1)

                lv = logit[pp][:, 0:NG * T].rearrange("p (g t) -> p g t", g=NG)

                def mask_and_group_max():
                    dve.wait_ge(logit_done, NG * it)
                    dve.tensor_tensor(lv[:, :, 0:LAGS], lv[:, :, 0:LAGS], maskc[:, :, :], ALU.min).then_inc(masked, 1)
                    dve.wait_ge(masked, it)
                    dve.tensor_reduce(t1[:, :], lv.rearrange("p g t -> p t g"), AX.X, ALU.max).then_inc(gmax_ready, 1)

                def lag_max():
                    ready("maxT")
                    m = W[BANK["maxT"]][:, :].rearrange("p (a u h) -> p a h u", a=TT, u=8)
                    dve.tensor_reduce(max2[:, :].rearrange("p (a h) -> p a h", a=TT), m, AX.X,
                                      ALU.max).then_inc(w_free[BANK["maxT"]], 1)

                def subtract_max():
                    ready("maxB")
                    dve.tensor_tensor(lv, lv, W[BANK["maxB"]][:, :].unsqueeze(1).to_broadcast([P, NG, T]),
                                      ALU.subtract).then_inc(w_free[BANK["maxB"]], 1)

                def evict(tt):
                    name = f"ev{tt}b"
                    ready(name)
                    wait(dve, z_written[(tt - 2) % TT], 16 * (pb_ + 1 if tt >= 2 else pb_))
                    src = W[BANK[name]][:, :].rearrange("p (g u h) -> p g u h", g=4, u=8)
                    dst = ev[:, tt % 2, :, 32:64].rearrange("p h (g u) -> p g u h", g=4)
                    dve.tensor_copy(dst, src).then_inc(w_free[BANK[name]], 1)

                def normalise(i):
                    w = W[BANK[f"heads{i}"]]
                    dve.wait_ge(band_used, NB * pb_ + 4 * i + 4)
                    dve.reciprocal(t1[:, 0:256], w[:, 256:512]).then_inc(recip_done, 1)
                    dve.wait_ge(recip_done, 2 * pb_ + i + 1)
                    dve.tensor_tensor(t2[:, 256 * i:256 * i + 256], w[:, 0:256], t1[:, 0:256],
                                      ALU.mult).then_inc(w_free[BANK[f"heads{i}"]], 1)

                def residual():
                    ready("cproj")
                    dve.wait_ge(xr_in, 16 * it)
                    r = res[:, :, :].rearrange("p a c -> p (a c)")
                    dve.tensor_tensor(r, W[BANK["cproj"]][:, :], r, ALU.add).then_inc(w_free[BANK["cproj"]], 1)
                    dve.wait_ge(w_free[BANK["cproj"]], use("cproj") + 1)
                    for a in range(TT):
                        dve.bn_stats(st[:, a, :], res[:, a, :]).then_inc(stat_done, 1)
                    dve.wait_ge(stat_done, 4 * it)
                    dve.tensor_copy(mark_[:, 0:1], st[:, 0, 0:1])
                    for a in range(TT):
                        dve.bn_aggr(mv[:, a, :], st[:, a, :]).then_inc(var_ready, 1)

                def first_norm():
                    dve.wait_ge(rstd_ready, it)
                    wait(dve, res2_ready, it - 1)
                    for a in range(TT):
                        dve.tensor_scalar(y[:, a, :], res[:, a, :], mv[:, a, 0:1], rstd[:, a:a + 1], ALU.subtract,
                                          ALU.mult).then_inc(y_ready, 1)

                def gate(hb):
                    dve.wait_ge(tanh_gate, KB * mb + hb + 1)
                    hrow = hid1[:, hb, :]
                    dve.scalar_tensor_tensor(out=hrow, in0=hrow, scalar=1.0, in1=W[BANK[f"gate{hb}"]][:, :], op0=ALU.add,
                                             op1=ALU.mult).then_inc(w_free[BANK[f"gate{hb}"]], 1)
                    dve.wait_ge(w_free[BANK[f"gate{hb}"]], use(f"gate{hb}") + 1)
                    ready(f"up{hb}")
                    dve.scalar_tensor_tensor(out=hrow, in0=hrow, scalar=s12[:, hb:hb + 1], in1=W[BANK[f"up{hb}"]][:, :],
                                             op0=ALU.mult, op1=ALU.mult).then_inc(w_free[BANK[f"up{hb}"]], 1)

                def mlp_residual():
                    ready("mlpout")
                    wait(dve, out_done, 16 * mb)
                    src = W[BANK["mlpout"]][:, :].rearrange("p (a c) -> p a c", a=TT)
                    dve.tensor_tensor(res2[:, :, :], src, w3sb[:, :].unsqueeze(1).to_broadcast([P, TT, C]),
                                      ALU.mult).then_inc(w_free[BANK["mlpout"]], 1)
                    dve.wait_ge(w_free[BANK["mlpout"]], use("mlpout") + 1)
                    dve.tensor_tensor(res2[:, :, :], res2[:, :, :], y[:, :, :], ALU.add).then_inc(res2_ready, 1)
                    dve.wait_ge(res2_ready, mb + 1)
                    for a in range(TT):
                        dve.bn_stats(st2[:, a, :], res2[:, a, :]).then_inc(stat2_done, 1)
                    dve.wait_ge(stat2_done, 4 * (mb + 1))
                    dve.tensor_copy(mark_[:, 1:2], st2[:, 0, 0:1])
                    for a in range(TT):
                        dve.bn_aggr(mv2[:, a, :], st2[:, a, :]).then_inc(var2_ready, 1)

                def second_norm():
                    dve.wait_ge(rstd2_ready, mb + 1)
                    for a in range(TT):
                        dve.tensor_scalar(res2[:, a, :], res2[:, a, :], mv2[:, a, 0:1], rstd2[:, a:a + 1], ALU.subtract,
                                          ALU.mult).then_inc(out_ready, 1)

                for k in range(NSLOT):
                    if pair_ and k < NCH and k % 4 == 0:
                        differences(DMG, k)
                    if att and k == 0:
                        combine(pb_, pp, NG - 1)
                    if pair_ and k >= LAG_B:
                        differences(BOND, k - LAG_B)
                    if pair_ and k % 4 == 3 and k >= 7:
                        combine(it, par, k // 4 - 1)
                    if mlp and k in GATE_DVE:
                        gate(GATE_DVE.index(k))
                    if mlp and k == 29:
                        mlp_residual()
                    if mlp and k == 32:
                        second_norm()
                    if att and k == 0:
                        mask_and_group_max()
                    if att and k == 4:
                        lag_max()
                    if att and k == 8:
                        subtract_max()
                    if att and k in (14, 16, 18, 20):
                        evict((k - 14) // 2)
                    if att and k == 26:
                        normalise(0)
                    if att and k == 31:
                        normalise(1)
                    if att and k == 33:
                        residual()
                if att:
                    first_norm()

            iterations(dve, body)

        @block.scalar
        def _(act):
            def body(it, par, pair_, att, mlp, nxt):
                pb_, pp, mb = it - 1, 1 - par, it - 2
                use = lambda name: bank_use(it, att, mlp, name)
                use_ready = lambda name: bank_use(it, att, mlp, name, COUNTED_BY_BLOCKS)

                def ready(name):
                    act.wait_ge(w_ready[BANK[name]], use_ready(name) + 1)

                def gelu(kind, c):
                    n = ACT_INDEX[(kind, c)]
                    g, half, pr, t0, w = chunk_parts(c)
                    wait(act, g_used, NACT * it + n - G_RING + 1)
                    if (kind, c) in DVE_CHUNKS:
                        m = DVE_CHUNKS.index((kind, c))
                        act.wait_ge(zv_ready, NDVE * it + m + 1)
                        z = zv[:, m % ZV_RING, 0:4 * w]
                    else:
                        m = POOL_CHUNKS.index((kind, c))
                        act.wait_ge(zp_ready, NPOOL * it + m + 1)
                        z = zp[:, m % ZP_RING, 0:4 * w]
                    bias = cols[:, 2:3] if kind == DMG else 0.0
                    act.activation(gl[:, n % G_RING, 0:4 * w], z, ACT.Gelu, bias=bias).then_inc(g_ready, 1)

                def damage_tanh(g):
                    act.wait_ge(g_used, NACT * it + ACT_INDEX[(DMG, 4 * g + 3)] + 1)
                    wait(act, logit_done, NG * it + g)
                    act.activation(th[:, 8 * g:T], LD[:, 8 * g:T], ACT.Tanh, bias=bcol[:, 0:1],
                                   scale=0.5).then_inc(tanh_done, 1)

                def copy_max():
                    ready("maxTT")
                    act.activation(t2[0:H, :], W[BANK["maxTT"]][0:H, :], ACT.Copy).then_inc(w_free[BANK["maxTT"]], 1)

                def exponent():
                    act.wait_ge(w_free[BANK["maxB"]], use("maxB") + 1)
                    v = logit[pp][:, 0:NG * T]
                    act.activation(v, v, ACT.Exp).then_inc(exp_done, 1)

                def evict(tt):
                    name = f"ev{tt}a"
                    ready(name)
                    wait(act, z_written[(tt - 2) % TT], 16 * (pb_ + 1 if tt >= 2 else pb_))
                    src = W[BANK[name]][:, :].rearrange("p (g u h) -> p g u h", g=4, u=8)
                    dst = ev[:, tt % 2, :, 0:32].rearrange("p h (g u) -> p g u h", g=4)
                    act.activation(dst, src, ACT.Copy).then_inc(w_free[BANK[name]], 1)

                def values(j):
                    name = f"val{j}"
                    ready(name)
                    for i in range(2):
                        wait(act, band_used, NB * pb_ + 2 * j - 1 + i)
                        base = vpad[:, i, 0, 0, 0:8]
                        dst = bass.AP(vpad, base.offset, [list(base.ap[0]), [128, 4], [40, 4], [1, HS]])
                        src = W[BANK[name]][:, P * i:P * i + P].rearrange("p (q h e) -> p q h e", q=4, h=4)
                        act.activation(dst, src, ACT.Copy)\
                           .then_inc(vpad_even if i == 0 else w_free[BANK[name]], 1)

                def y_transposed():
                    ready("yT")
                    act.activation(yT[:, :], W[BANK["yT"]][:, :], ACT.Copy).then_inc(w_free[BANK["yT"]], 1)

                def gate_tanh(hb):
                    ready(f"gate{hb}")
                    wait(act, res2_ready, mb)
                    act.activation(hid1[:, hb, :], W[BANK[f"gate{hb}"]][:, :], ACT.Tanh,
                                   scale=s1h[:, hb:hb + 1]).then_inc(tanh_gate, 1)

                def hidden(layer, ob):
                    name = f"h{layer}_{ob}"
                    ready(name)
                    dst, sc = ((hid2, sh1), (hid1, sh2))[layer - 1]
                    act.activation(dst[:, ob, :], W[BANK[name]][:, :], ACT.Gelu,
                                   scale=sc[:, ob:ob + 1]).then_inc(w_free[BANK[name]], 1)

                def copy_projection(b, i):
                    kind, half, bank = ((DMG, 1, PD), (DMG, 0, PD), (BOND, 0, PA[0]), (BOND, 1, PA[1]))[i]
                    act.wait_ge(proj_ready, 4 * b + i + 1)
                    act.activation(pair[1 - par][:, kind, half, LPAD:], bank[:, :], ACT.Copy)\
                       .then_inc(proj_copied, 1)

                for k in range(NSLOT):
                    if pair_ and k < NCH:
                        gelu(DMG, k)
                    if pair_ and k % 4 == 0 and k >= 4:
                        damage_tanh(k // 4 - 1)
                    if pair_ and k >= LAG_B:
                        gelu(BOND, k - LAG_B)
                    if mlp and k in GATE_ACT:
                        gate_tanh(GATE_ACT.index(k))
                    if att and k == 5:
                        copy_max()
                    if att and k == 9:
                        exponent()
                    if mlp and 12 <= k < 20 and k % 2 == 0:
                        hidden(1, (k - 12) // 2)
                    if att and k in (12, 14, 16, 18):
                        evict((k - 12) // 2)
                    if mlp and 20 <= k < 28 and k % 2 == 0:
                        hidden(2, (k - 20) // 2)
                    if att and k in VALUES_ACT:
                        values(VALUES_ACT.index(k))
                    if nxt and k in (30, 31, 33):
                        copy_projection(it + 1, {30: 0, 31: 1, 33: 2}[k])
                if nxt:
                    copy_projection(it + 1, 3)
                if att:
                    y_transposed()

            act.wait_ge(dve_const, DVE_ALL)
            for i in range(4):
                kind, half, bank = ((DMG, 1, PD), (DMG, 0, PD), (BOND, 0, PA[0]), (BOND, 1, PA[1]))[i]
                act.wait_ge(proj_ready, i + 1)
                act.activation(pair[0][:, kind, half, LPAD:], bank[:, :], ACT.Copy).then_inc(proj_copied, 1)
            iterations(act, body)

        @block.tensor
        def _(pe):
            def project(b, i):
                kind, half, bank = ((DMG, 1, PD), (DMG, 0, PD), (BOND, 0, PA[0]), (BOND, 1, PA[1]))[i]
                if i == 1:
                    pe.wait_ge(proj_copied, 4 * b + 1)
                elif not (isinstance(b, int) and b == 0):
                    last = {0: (DMG, NCH - 4), 2: (BOND, NCH - 3), 3: (BOND, NCH - 1)}[i]
                    pe.wait_ge(zv_ready, NDVE * (b - 1) + DVE_CHUNKS.index(last) + 1)
                pe.matmul(bank[:, :], wpair[:, 2 * kind + half, :], xTp[:, :], start=True,
                          stop=True).then_inc(proj_ready, 1)

            pe.wait_ge(setup_in, SETUP_DMAS * 16)
            pe.wait_ge(pool_const, POOL_CONSTS)
            pe.wait_ge(dve_const, DVE_A)
            pe.matmul(LB[:, 0:35], rep, wvec, start=True, stop=True).then_inc(pe_const, 1)
            pe.wait_ge(dve_const, DVE_A + 1)
            pe.matmul(LB[:, 64:64 + LAGS], wposrep, relt, start=True, stop=True).then_inc(pe_const, 1)
            pe.wait_ge(dve_const, DVE_A + 3)
            for f in range(2):
                for half in range(2):
                    mm = pe.matmul(LD[:, P * (2 * f + half):P * (2 * f + half) + P], wdt[:, half, :], bdg[:, f, :],
                                   start=True, stop=True)
            mm.then_inc(pe_const, 1)
            pe.wait_ge(dve_const, DVE_ALL)
            for i in range(4):
                project(0, i)

            def body(it, par, pair_, att, mlp, nxt):
                pb_, pp, mb = it - 1, 1 - par, it - 2
                use = lambda name: bank_use(it, att, mlp, name)
                use_ready = lambda name: bank_use(it, att, mlp, name, COUNTED_BY_BLOCKS)

                def free(name):
                    wait(pe, w_free[BANK[name]], use(name))
                    return W[BANK[name]]

                def done(name, mm):
                    mm.then_inc(w_ready[BANK[name]], 1)

                def contract(kind, c):
                    n = ACT_INDEX[(kind, c)]
                    g, half, pr, t0, w = chunk_parts(c)
                    bank = (LB, LD)[kind]
                    if c % 4 == 0:
                        wait(pe, (logit_done, tanh_done)[kind], NG * it + g)
                    pe.wait_ge(g_ready, NACT * it + n + 1)
                    gv = gl[:, n % G_RING, 0:4 * w].rearrange("p (i t) -> p i t", i=4)
                    for q in range(4):
                        mm = pe.matmul(bank[32 * q:32 * q + 32, t0:T], ctr[:, kind, 2 * pr + half, :], gv[:, 3 - q, :],
                                       start=(c % 4 == 0), stop=(c % 4 == 3))
                    mm.then_inc(g_used, 1)

                def max_transposed():
                    pe.wait_ge(gmax_ready, it)
                    w = free("maxT")
                    for a in range(TT):
                        mm = pe.transpose(w[:, P * a:P * a + P], t1[:, P * a:P * a + P], ident[:, :])
                    done("maxT", mm)

                def max_rows():
                    pe.wait_ge(w_free[BANK["maxT"]], use("maxT") + 1)
                    w = free("maxTT")
                    for a in range(TT):
                        mm = pe.transpose(w[0:H, P * a:P * a + P], max2[:, H * a:H * a + H], ident[:, :])
                    done("maxTT", mm)

                def max_broadcast():
                    pe.wait_ge(w_free[BANK["maxTT"]], use("maxTT") + 1)
                    w = free("maxB")
                    done("maxB", pe.matmul(w[:, :], selm[:, :], t2[0:H, :], start=True, stop=True))

                def weights_transposed(tt, i):
                    pe.wait_ge(shifted[tt % 2], 256 * pb_ + 128 * (tt // 2) + 128)
                    name = f"ev{tt}{'ab'[i]}"
                    w = free(name)
                    for g in range(4):
                        mm = pe.transpose(w[:, P * g:P * g + P], esh[:, tt % 2, 4 * i + g, :], ident[:, :])
                    done(name, mm)

                def value_rows(j):
                    name = f"val{j}"
                    pe.wait_ge(xv_in, 16 * it)
                    w = free(name)
                    for i in range(2):
                        s0 = 64 * (2 * j + i) + 1
                        mm = pe.matmul(w[:, P * i:P * i + P], xTv[:, s0:s0 + P], wval[:, :], start=True, stop=True)
                    done(name, mm)

                def banded(k):
                    if k % 4 == 0:
                        free(f"heads{k // 4}")
                    if k % 2 == 0:
                        pe.wait_ge(vpad_even, 4 * pb_ + k // 2 + 1)
                    else:
                        pe.wait_ge(w_free[BANK[f"val{k // 2}"]], use(f"val{k // 2}") + 1)
                    pe.wait_ge(band_in[k % 2], 64 * pb_ + 16 * (k // 2) + 16)
                    w = W[BANK["heads0"]]
                    for wt, c0 in ((vpad[:, k % 2, :, :, :], 0), (None, 256)):
                        t = slice(c0 + 64 * (k % 4), c0 + 64 * (k % 4) + 64)
                        for h in range(4):
                            for q in range(4):
                                lhs = ones[:, h, :] if wt is None else wt[:, q, h, :]
                                mm = pe.matmul(w[32 * q:32 * q + 32, t], lhs, band[:, k % 2, 4 * q + h, :],
                                               start=(h == 0), stop=(h == 3))
                    mm.then_inc(band_used, 1)

                def output_projection():
                    pe.wait_ge(w_free[BANK["heads1"]], use("heads1") + 1)
                    w = free("cproj")
                    for a in range(TT):
                        mm = pe.matmul(w[:, P * a:P * a + P], t2[:, P * a:P * a + P], wcp[:, :], start=True, stop=True)
                    done("cproj", mm)

                def y_transposed():
                    pe.wait_ge(y_ready, 4 * it)
                    w = free("yT")
                    for a in range(TT):
                        mm = pe.transpose(w[:, P * a:P * a + P], y[:, a, :], ident[:, :])
                    done("yT", mm)

                def gate_up(hb):
                    for name, wt in ((f"gate{hb}", w1t), (f"up{hb}", w2t)):
                        w = free(name)
                        done(name, pe.matmul(w[:, :], wt[:, P * hb:P * hb + P], yT[:, :], start=True, stop=True))

                def hidden(layer, ob, part):
                    name = f"h{layer}_{ob}"
                    src, wt = ((hid1, h1t), (hid2, h2t))[layer - 1]
                    if part == 0:
                        free(name)
                        if ob == 0:
                            last = ("up3", "h1_3")[layer - 1]
                            pe.wait_ge(w_free[BANK[last]], use(last) + 1)
                    w = W[BANK[name]]
                    for kb in range(2 * part, 2 * part + 2):
                        mm = pe.matmul(w[:, :], wt[:, kb, P * ob:P * ob + P], src[:, kb, :], start=(kb == 0),
                                       stop=(kb == KB - 1))
                    if part == 1:
                        done(name, mm)

                def mlp_out(part):
                    if part == 0:
                        free("mlpout")
                        pe.wait_ge(w_free[BANK["h2_3"]], use("h2_3") + 1)
                    w = W[BANK["mlpout"]]
                    for a in range(2 * part, 2 * part + 2):
                        for kb in range(KB):
                            mm = pe.matmul(w[:, P * a:P * a + P], hid1[:, kb, P * a:P * a + P], w3t[:, kb, :],
                                           start=(kb == 0), stop=(kb == KB - 1))
                    if part == 1:
                        done("mlpout", mm)

                for k in range(NSLOT):
                    if pair_ and k < NCH:
                        contract(DMG, k)
                    if mlp and k in GATE_PE and k != 2 and k != 7:
                        gate_up(GATE_PE.index(k))
                    if att and k == 2:
                        max_transposed()
                    if att and k == 4:
                        max_rows()
                    if mlp and 10 <= k < 18:
                        hidden(1, (k - 10) // 2, k % 2)
                    if mlp and 18 <= k < 26:
                        hidden(2, (k - 18) // 2, k % 2)
                    if mlp and 26 <= k < 28:
                        mlp_out(k - 26)
                    if pair_ and k >= LAG_B:
                        contract(BOND, k - LAG_B)
                    if att and k == 6:
                        max_broadcast()
                    if mlp and k in (2, 7):
                        gate_up(GATE_PE.index(k))
                    if att and 11 <= k < 19:
                        weights_transposed((k - 11) // 2, (k - 11) % 2)
                    if att:
                        for block_ in BLOCKS_PE.get(k, ()):
                            banded(block_)
                    if att and k in VALUES_PE:
                        value_rows(VALUES_PE.index(k))
                    if nxt and k == 29:
                        pe.wait_ge(xp_in, 16 * (it + 1))
                        project(it + 1, 0)
                    if nxt and k == 30:
                        project(it + 1, 1)
                    if att and k == 32:
                        output_projection()
                    if nxt and k == 32:
                        project(it + 1, 2)
                if nxt:
                    project(it + 1, 3)
                if att:
                    y_transposed()

            iterations(pe, body)


GATE_PE = (0, 2, 5, 7)
GATE_ACT = (1, 3, 6, 8)
GATE_DVE = (3, 5, 8, 10)
VALUES_PE = (19, 21, 25, 27)
VALUES_ACT = (20, 22, 26, 28)
BLOCKS_PE = {20: (0,), 21: (1,), 23: (2,), 24: (3,), 26: (4,), 27: (5,), 29: (6, 7)}
SETUP_DMAS = 22
POOL_CONSTS = 13
DVE_ZERO = 2
DVE_A = 16
DVE_ALL = DVE_A + 1 + 2 + 8 + 2


_INS = ["xT", "x", "W_dispT", "W_val", "relT", "W_strain", "W_pos", "W_bond", "W_dmg", "b_dmg", "W_dmg_out",
        "b_dmg_out", "W_cproj", "w1T", "w1_s", "w2T", "w2_s", "h1T", "h1_s", "h2T", "h2_s", "w3T", "w3_s"]


def kernel(**inputs):
    import numpy as np
    import concourse.bacc as bacc
    from concourse.bass_utils import run_bass_kernel_spmd

    a = {k: np.asarray(v) for k, v in inputs.items()}
    x = a["L0_attn_x"]
    given = {
        "xT": x.transpose(2, 0, 1).reshape(x.shape[2], -1), "x": x,
        "W_dispT": a["L0_attn_W_disp"].T, "relT": a["L0_attn_rel_pos_emb"].T,
        **{n: a[f"L0_attn_{n}"] for n in ("W_val", "W_strain", "W_pos", "W_bond", "W_dmg", "b_dmg", "W_dmg_out",
                                          "b_dmg_out", "W_cproj")},
        **{f"{n}T": a[f"L0_ffn_{n}_w"].T for n in ("w1", "w2", "h1", "h2", "w3")},
        **{f"{n}_s": a[f"L0_ffn_{n}_s"].reshape(-1, P).T for n in ("w1", "w2", "h1", "h2")},
        "w3_s": a["L0_ffn_w3_s"],
    }
    nc = bacc.Bacc("TRN2", target_bir_lowering=False, num_devices=1)
    arrays, args = {}, []
    for name in _INS:
        v = np.ascontiguousarray(given[name])
        arrays[f"in_{name}"] = v
        args.append(nc.dram_tensor(f"in_{name}", v.shape, mybir.dt.from_np(v.dtype), kind="ExternalInput").ap())
    args.append(nc.dram_tensor("out_0", x.shape, F32, kind="ExternalOutput").ap())
    block_kernel(nc, *args)
    r = run_bass_kernel_spmd(nc, [arrays], core_ids=[0])
    return r.results[0]["out_0"]
```

```python
from contextlib import ExitStack

import concourse.bass as bass
from concourse import mybir

F32 = mybir.dt.float32
ALU = mybir.AluOpType
ACT = mybir.ActivationFunctionType
AX = mybir.AxisListType

P = 128
H = 16
HH = 8
BD = 16
HS = 8
LAGS = 64
NG = 8
LPAD = 8
LN_EPS = 1e-5
MASKED = -1e30
NCH = 4 * NG
LAG_B = 1
NSLOT = NCH + LAG_B
NB = 512 // 64
ZROW = 128
BOND, DMG = 0, 1
BATCHES = 16


def act_order():
    order = []
    for k in range(NSLOT):
        if k < NCH:
            order.append((DMG, k))
        if k >= LAG_B:
            order.append((BOND, k - LAG_B))
    return order


ACT_ORDER = act_order()
ACT_INDEX = {c: n for n, c in enumerate(ACT_ORDER)}
NACT = len(ACT_ORDER)
DVE_DAMAGE = (0, 12, 20, 24)
DVE_CHUNKS = [c for c in ACT_ORDER if c[0] == BOND or c[1] in DVE_DAMAGE]
POOL_CHUNKS = [c for c in ACT_ORDER if c not in DVE_CHUNKS]
NDVE, NPOOL = len(DVE_CHUNKS), len(POOL_CHUNKS)
ZV_RING, ZP_RING, G_RING = 2, 2, 4

STEP = NSLOT
V1, V2, V3, V4 = NSLOT, 2 * NSLOT, 3 * NSLOT, 4 * NSLOT
PE_MLP = {
    "yT": V3 + 1, "gate0": V3 + 2, "up0": V3 + 2, "gate1": V3 + 4, "up1": V3 + 4, "gate2": V3 + 5, "up2": V3 + 5,
    "gate3": V3 + 11, "up3": V3 + 11, "h1_0": V3 + 12, "h1_1": V3 + 13, "h1_2": V3 + 15, "h1_3": V3 + 16,
    "h2_0": V3 + 19, "h2_1": V3 + 20, "h2_2": V3 + 23, "h2_3": V3 + 24, "mlpout": V3 + 27,
}
PE_MLP_SECOND = {
    "h1_0": V3 + 12, "h1_1": V3 + 13, "h1_2": V3 + 15, "h1_3": V3 + 18, "h2_0": V3 + 20, "h2_1": V3 + 21,
    "h2_2": V3 + 23, "h2_3": V3 + 24, "mlpout": V3 + 29,
}
PE_ATT = {
    "cproj": V2 + 4, "maxT": V1 + 7, "maxTT": V1 + 8, "maxB": V1 + 11, "val0": V1 + 15, "ev0a": V1 + 17,
    "ev0b": V1 + 18, "ev1a": V1 + 18, "ev1b": V1 + 19, "ev2a": V1 + 20, "ev2b": V1 + 22, "ev3a": V1 + 23,
    "ev3b": V1 + 26, "val1": V1 + 27, "heads0": V1 + 26, "heads1": V1 + 32,
}
PE_BLOCK = [V1 + 26, V1 + 28, V1 + 29, V1 + 29, V1 + 32, V1 + 32, V2 + 2, V2 + 2]
PE_PROJ = [-STEP + 24, -STEP + 29, -STEP + 29, -STEP + 31]
BANK = {
    "yT": 1, "gate0": 0, "up0": 1, "gate1": 2, "up1": 1, "gate2": 0, "up2": 1, "gate3": 0, "up3": 1, "h1_0": 0,
    "h1_1": 1, "h1_2": 0, "h1_3": 1, "h2_0": 0, "h2_1": 2, "h2_2": 0, "h2_3": 1, "mlpout": 0, "cproj": 2,
    "maxT": 2, "maxTT": 2, "maxB": 2, "val0": 2, "val1": 2, "ev0a": 2, "ev0b": 0, "ev1a": 2, "ev1b": 2, "ev2a": 1,
    "ev2b": 1, "ev3a": 2, "ev3b": 2, "heads0": 1, "heads1": 2,
}
ACT_AT = {
    "tanh": [4, 8, 12, 16, 20, 24, 28, V1 + 0], "proj": [-STEP + 29, -STEP + 31], "copy_max": V1 + 9,
    "exp": V1 + 16, "evict_a": [V1 + 18, V1 + 19, V1 + 22, V1 + 24], "evict_b": [V1 + 19, V1 + 24],
    "values": [V1 + 17, V1 + 32], "yT": V3 + 2, "gate": [V3 + 3, V3 + 5, V3 + 7, V3 + 11],
    "h1": [V3 + 14, V3 + 15, V3 + 18, V3 + 19], "h2": [V3 + 22, V3 + 22, V3 + 26, V3 + 26],
}
DVE_AT = {
    "combine": [7, 10, 14, 17, 22, 26, 30, V1 + 1], "group_max": [V1 + 4, V1 + 4, V1 + 4, V1 + 8],
    "lag_max": V1 + 9, "subtract": [V1 + 14, V1 + 14, V1 + 15, V1 + 15], "evict_b": [V1 + 21, V1 + 28],
    "normalise": [V2 + 0, V2 + 5], "residual": V2 + 8, "norm1": V2 + 32,
    "gate": [V3 + 5, V3 + 6, V3 + 11, V3 + 12], "mlp_residual": V3 + 31, "norm2": V4 + 7, "copy_a": [1, 3],
}
POOL_AT = {"rstd1": V2 + 10, "rstd2": V4 + 0}
PE_ORDER, PE_STAGE = {}, {}
for _place, _table in enumerate((PE_MLP, PE_ATT)):
    for _i, (_name, _v) in enumerate(_table.items()):
        PE_ORDER[_name] = (_v % STEP, _place, _i)
        PE_STAGE[_name] = _v // STEP
COUNTED_BY_BLOCKS = ("heads0", "heads1")
LAST_STAGE = 4


def bank_use(b, name, skip=()):
    it = b + PE_STAGE[name]
    others = [n for n in PE_ORDER if BANK[n] == BANK[name] and n not in skip]
    if isinstance(it, int):
        return sum(min(max(it - PE_STAGE[n] + (PE_ORDER[n] < PE_ORDER[name]), 0), BATCHES) for n in others)
    return len(others) * it + sum((PE_ORDER[n] < PE_ORDER[name]) - PE_STAGE[n] for n in others)


def block_kernel(nc, xT, x, W_dispT, W_val, relT, W_strain, W_pos, W_bond, W_dmg, b_dmg, W_dmg_out, b_dmg_out,
                 W_cproj, w1T, w1_s, w2T, w2_s, h1T, h1_s, h2T, h2_s, w3T, w3_s, out):
    B, T, C = x.shape
    DH = w1T.shape[1]
    KB = DH // P
    TT = T // P
    assert B == BATCHES and C == P and T == 512 and H * HS == C

    ZH = (T + LAGS) * ZROW
    scratch = nc.dram_tensor("band_scratch", (H * ZH,), F32)

    ctx = ExitStack()
    with ctx:
        def sb(name, shape):
            return ctx.enter_context(nc.sbuf_tensor(name, shape, F32))

        def pb(name):
            return ctx.enter_context(nc.psum_tensor(name, [P, 512], F32))

        def sem(name):
            return ctx.enter_context(nc.semaphore(name))

        zv = sb("zv", [P, ZV_RING, 2048])
        zp = sb("zp", [P, ZP_RING, 2048])
        gl = sb("gl", [P, G_RING, 2048])
        LFLAT = NG * T + LAGS
        logit = [sb(f"logit{i}", [P, LFLAT]) for i in range(2)]
        esh = sb("esh", [P, 2, NG, P])
        ev = sb("ev", [P, 2, H, LAGS])
        band = sb("band", [P, 2, H, 64])
        AW = LPAD + T
        pair = [sb(f"pair{i}", [P, 2, 2, AW]) for i in range(2)]
        maxrow = band[0:H, 0, 0:T // 64, :].rearrange("h a t -> h (a t)")
        w1t = sb("w1t", [P, DH])
        w2t = sb("w2t", [P, DH])
        h1t = sb("h1t", [P, KB, DH])
        h2t = sb("h2t", [P, KB, DH])
        w3t = sb("w3t", [P, KB, P])
        wpair = sb("wpair", [P, 4, P])
        wval = sb("wval", [P, P])
        wcp = sb("wcp", [P, P])
        ident = sb("ident", [P, P])
        selm = sb("selm", [H, P])
        ones = sb("ones", [P, 4, 32])
        ctr = sb("ctr", [P, 2, 4, 32])
        maskt = sb("maskt", [P, LAGS])
        w3sb = sb("w3sb", [P, P])
        xTp = sb("xTp", [P, T])
        xTv = sb("xTv", [P, LAGS + T + LAGS])
        hid1 = sb("hid1", [P, KB, T])
        hid2 = sb("hid2", [P, KB, T])
        th = sb("th", [P, T])
        yT = hid2[:, KB - 1, :]
        y = sb("y", [P, TT, C])
        res = sb("res", [P, TT, C])
        res2 = sb("res2", [P, TT, C])
        t1 = sb("t1", [P, T])
        t2 = sb("t2", [P, T])
        vpad = sb("vpad", [P, 4, 4, 4, 32])
        max2 = sb("max2", [P, TT * H])
        st = sb("st", [P, TT, 6])
        mv = sb("mv", [P, TT, 2])
        rstd = sb("rstd", [P, TT])
        st2 = sb("st2", [P, TT, 6])
        mv2 = sb("mv2", [P, TT, 2])
        rstd2 = sb("rstd2", [P, TT])
        ve = sb("ve", [P, TT])
        ve2 = sb("ve2", [P, TT])
        mhalf = sb("mhalf", [P, TT])
        epst = sb("epst", [P, TT])
        mark_ = sb("mark_", [P, 2])
        relR = sb("relR", [P, LAGS])
        bcol = sb("bcol", [P, 1])
        boraw = sb("boraw", [P, 1])
        s1 = sb("s1", [P, KB])
        s2 = sb("s2", [P, KB])
        s1h = sb("s1h", [P, KB])
        s12 = sb("s12", [P, KB])
        sh1 = sb("sh1", [P, KB])
        sh2 = sb("sh2", [P, KB])
        m8 = sb("m8", [P, HH])
        cols = sb("cols", [P, 35])

        PA = [pb("PA0"), pb("PA1")]
        PD = pb("PD")
        LB = pb("LB")
        LD = pb("LD")
        W = [pb(f"W{i}") for i in range(3)]

        setup_in = sem("setup_in")
        weights_in = sem("weights_in")
        scales_made = sem("scales_made")
        later_zero = sem("later_zero")
        pool_const = sem("pool_const")
        dve_const = sem("dve_const")
        pe_const = sem("pe_const")
        scratch_zero = sem("scratch_zero")
        xp_in = sem("xp_in")
        xv_in = sem("xv_in")
        xr_in = sem("xr_in")
        proj_ready = sem("proj_ready")
        d_copied = sem("d_copied")
        a_copied = sem("a_copied")
        zv_ready = sem("zv_ready")
        zp_ready = sem("zp_ready")
        g_ready = sem("g_ready")
        g_used = sem("g_used")
        tanh_done = sem("tanh_done")
        logit_done = sem("logit_done")
        masked = sem("masked")
        gmax_ready = sem("gmax_ready")
        exp_done = sem("exp_done")
        shifted = [sem(f"shifted{i}") for i in range(2)]
        z_written = [sem(f"z_written{i}") for i in range(TT)]
        band_in = [sem(f"band_in{i}") for i in range(2)]
        band_used = sem("band_used")
        stat_done = sem("stat_done")
        var_ready = sem("var_ready")
        res2_ready = sem("res2_ready")
        rs_step = sem("rs_step")
        rs2_step = sem("rs2_step")
        rstd_ready = sem("rstd_ready")
        y_ready = sem("y_ready")
        tanh_gate = sem("tanh_gate")
        stat2_done = sem("stat2_done")
        var2_ready = sem("var2_ready")
        rstd2_ready = sem("rstd2_ready")
        out_ready = sem("out_ready")
        out_done = sem("out_done")
        recip_done = sem("recip_done")
        w_ready = [sem(f"w_ready{i}") for i in range(3)]
        w_free = [sem(f"w_free{i}") for i in range(3)]

        block = ctx.enter_context(nc.Block())

        def iterations(eng, body):
            for it in range(5):
                body(it, it % 2)
            with eng.Fori(0, (B - 6) // 2) as i:
                body(2 * i + 5, 1)
                body(2 * i + 6, 0)
            for it in range(B - 1, B + LAST_STAGE + 1):
                body(it, it % 2)

        def exists(it, stage):
            return not isinstance(it, int) or 0 <= it - stage < B

        def at(k, it, placed):
            return placed % STEP == k and exists(it, placed // STEP)

        def wait(eng, s, value):
            if not (isinstance(value, int) and value <= 0):
                eng.wait_ge(s, value)

        def chunk_parts(c):
            g, half, par = c // 4, (c // 2) % 2, c % 2
            return g, half, par, 8 * g, T - 8 * g

        def shifted_rows(tile, kind, half, par, n):
            full = tile[:, kind, half, :]
            start = full.offset + LPAD - par - 6
            return bass.AP(tile, start, [list(full.ap[0]), [2, 4], [1, n]])

        wvec = gl[0:16, 0, 0:35]
        wposr = gl[0:16, 0, 64:80]
        wposrep = gl[0:16, 0, 128:256]
        relt = gl[0:16, 0, 256:320]
        rep = gl[0:16, 0, 384:512]
        wdt = gl[:, 1, 0:256].rearrange("p (a c) -> p a c", a=2)
        bdg = gl[:, 2, 0:256].rearrange("p (f c) -> p f c", f=2)
        big = gl[:, 3, 0:LAGS]

        @block.sync
        def _(sp):
            def load(dst, src):
                sp.dma_start(dst, src).then_inc(setup_in, 16)

            col = lambda v: v.rearrange("(a b) -> a b", b=1)
            load(wvec[:, 0:1], W_bond)
            load(wvec[:, 1:2], W_dmg_out)
            load(wvec[:, 2:3], col(b_dmg))
            load(wvec[:, 3:19], W_strain)
            load(wvec[:, 19:35], W_dmg)
            load(wdt, W_dispT.rearrange("(a p) c -> p a c", p=P))
            load(wposr[:, :], W_pos)
            load(relt[:, :], relT)
            load(xTp[:, :], xT[:, 0:T])
            load(boraw[:, :], col(b_dmg_out).partition_broadcast(P).rearrange("p a b -> p (a b)"))
            late = lambda dst, src: sp.dma_start(dst, src).then_inc(weights_in, 16)
            late(wval[:, :], W_val)
            late(wcp[:, :], W_cproj)
            late(w1t[:, :], w1T)
            late(w2t[:, :], w2T)
            late(h1t[:, :, :], h1T.rearrange("(k p) o -> p k o", p=P))
            late(h2t[:, :, :], h2T.rearrange("(k p) o -> p k o", p=P))
            late(w3t[:, :, :], w3T.rearrange("(k p) o -> p k o", p=P))
            for dst, src in ((s1, w1_s), (s2, w2_s), (sh1, h1_s), (sh2, h2_s)):
                late(dst[:, :], src)
            late(w3sb[:, :], w3_s.partition_broadcast(P))
            sp.wait_ge(dve_const, DVE_ZERO)
            per = H * ZH // P
            zero = scratch[:].rearrange("(p n) -> p n", p=P)
            for q in range(4):
                sp.dma_start(zero[:, q * per // 4:(q + 1) * per // 4],
                             logit[0][:, 0:per // 4]).then_inc(scratch_zero, 16)

            def shift(v, pp, tt):
                if tt == 0:
                    sp.wait_ge(exp_done, v["batch"])
                if tt >= 2:
                    sp.wait_ge(w_ready[BANK[f"ev{tt - 2}b"]], v["transposed"][tt - 2])
                src = logit[pp][:, :]
                for u8 in range(8):
                    rows = src[16 * u8:16 * u8 + 16, :]
                    view = bass.AP(logit[pp], rows.offset + u8 + P * tt, [list(rows.ap[0]), [T + 8, NG], [1, P]])
                    sp.dma_start(esh[16 * u8:16 * u8 + 16, tt % 2, :, :], view).then_inc(shifted[tt % 2], 16)

            def scratch_write(v, tt):
                sp.wait_ge(w_free[BANK[f"ev{tt}b"]], v["evicted"][tt])
                dst = bass.AP(scratch, (LAGS + P * tt) * ZROW, [[ZROW, P], [ZH, H], [1, LAGS]])
                sp.dma_start(dst, ev[:, tt % 2, :, :]).then_inc(z_written[tt], 16)

            def band_read(v, k):
                if k >= 2:
                    sp.wait_ge(band_used, v["block"][k])
                for tt in range(max(0, (k - 1) // 2), k // 2 + 1):
                    sp.wait_ge(z_written[tt], v["stored"])
                src = bass.AP(scratch, (LAGS + 64 * k - 63) * (ZROW - 1) + LAGS + 64 * k,
                              [[ZROW - 1, P], [ZH, H], [1, 64]])
                sp.dma_start(band[:, k % 2, :, :], src).then_inc(band_in[k % 2], 16)

            def x_rows(src, b):
                if isinstance(b, int):
                    return src[b:b + 1, :, :].rearrange("b (a p) c -> p (b a) c", p=P)
                return src[bass.ds(b, 1), :, :].rearrange("b (a p) c -> p (b a) c", p=P)

            def x_cols(col):
                return xT[:, bass.ds(col, T)]

            def store_output(v):
                sp.wait_ge(out_ready, v["normed2"])
                sp.dma_start(x_rows(out, v["out_row"]), res2[:, :, :]).then_inc(out_done, 16)

            def body(it, par):
                store_stage, store_early = DVE_AT["norm2"] // STEP, DVE_AT["norm2"] % STEP < 14
                att, store, nxt = exists(it, 1), exists(it, store_stage), exists(it, -1)
                b, pp = it - 1, (par + 1) % 2

                def fixed(value):
                    return value if isinstance(value, int) else sp.snap(value)

                v = {}
                if nxt:
                    v["made"] = fixed(4 * (it + 1))
                    next_cols = fixed((it + 1) * T)
                if att:
                    v["batch"] = fixed(b + 1)
                    v["normed"] = fixed(4 * b)
                    v["multiplied"] = fixed(NB * b)
                    v["stored"] = fixed(16 * (b + 1))
                    v["evicted"] = [fixed(bank_use(b, f"ev{t}b") + 1) for t in range(TT)]
                    v["transposed"] = [fixed(bank_use(b, f"ev{t}b", COUNTED_BY_BLOCKS) + 1) for t in range(2)]
                    v["block"] = [fixed(NB * b + k - 1) for k in range(NB)]
                    this_cols, this_row = fixed(b * T), fixed(b)
                if store:
                    v["normed2"] = fixed(4 * (it - store_stage + 1))
                    v["out_row"] = fixed(it - store_stage)
                if nxt:
                    sp.wait_ge(proj_ready, v["made"])
                    sp.dma_start(xTp[:, :], x_cols(next_cols)).then_inc(xp_in, 16)
                if store and store_early:
                    store_output(v)
                if att:
                    wait(sp, band_used, v["multiplied"])
                    if isinstance(it, int) and it == 1:
                        sp.wait_ge(later_zero, 1)
                    sp.dma_start(xTv[:, LAGS:LAGS + T], x_cols(this_cols)).then_inc(xv_in, 16)
                    if isinstance(it, int) and it == 1:
                        sp.wait_ge(scratch_zero, 64)
                    shift(v, pp, 0)
                    shift(v, pp, 1)
                    scratch_write(v, 0)
                    shift(v, pp, 2)
                    scratch_write(v, 1)
                    shift(v, pp, 3)
                    scratch_write(v, 2)
                    band_read(v, 0)
                    band_read(v, 1)
                    scratch_write(v, 3)
                    for k in range(2, 6):
                        band_read(v, k)
                if store and not att and not store_early:
                    store_output(v)
                if att:
                    for k in range(6, NB):
                        band_read(v, k)
                    if store and not store_early:
                        store_output(v)
                    wait(sp, y_ready, v["normed"])
                    sp.dma_start(res[:, :, :], x_rows(x, this_row)).then_inc(xr_in, 16)

            iterations(sp, body)
            sp.wait_ge(out_done, 16 * B)

        @block.gpsimd
        def _(pool):
            step = [0]

            def link(ins):
                step[0] += 1
                ins.then_inc(pool_const, 1)
                pool.wait_ge(pool_const, step[0])

            link(pool.memset(ident[:, :], 0.0))
            link(pool.affine_select(out=ident[:, :], in_=ident[:, :], compare_op=ALU.not_equal, fill=1.0, base=0,
                                    pattern=[[-1, P]], channel_multiplier=1))
            link(pool.memset(rep, 0.0))
            link(pool.affine_select(out=rep.rearrange("d (h o) -> d h o", h=HH), in_=rep.rearrange("d (h o) -> d h o", h=HH),
                                    compare_op=ALU.not_equal, fill=1.0, base=0, pattern=[[0, HH], [-1, BD]],
                                    channel_multiplier=1))
            link(pool.memset(selm[:, :], 0.0))
            sv = selm[:, :].rearrange("h (l g) -> h l g", l=8)
            link(pool.affine_select(out=sv, in_=sv, compare_op=ALU.not_equal, fill=1.0, base=0,
                                    pattern=[[0, 8], [-1, H]], channel_multiplier=1))
            link(pool.memset(m8[:, :], 1.0))
            link(pool.affine_select(out=m8[:, :], in_=m8[:, :], compare_op=ALU.is_ge, fill=0.0, base=0,
                                    pattern=[[-BD, HH]], channel_multiplier=1))
            link(pool.affine_select(out=m8[:, :], in_=m8[:, :], compare_op=ALU.is_ge, fill=0.0, base=BD - 1,
                                    pattern=[[BD, HH]], channel_multiplier=-1))
            link(pool.memset(big, 3e38))
            link(pool.affine_select(out=maskt[:, :], in_=big, compare_op=ALU.is_ge, fill=MASKED,
                                    base=15 - 16 * (LAGS - 8), pattern=[[16, LAGS]], channel_multiplier=-1))
            link(pool.memset(mhalf[:, :], -0.5))
            link(pool.memset(epst[:, :], LN_EPS))
            assert step[0] == POOL_CONSTS
            pool.memset(xTv[:, :], 0.0).then_inc(later_zero, 1)
            pool.memset(vpad[:, :, :, :, :], 0.0).then_inc(later_zero, 1)
            pool.memset(logit[1][:, :], 0.0).then_inc(later_zero, 1)

            def body(it, par):
                def differences(n, c):
                    g, half, pr, t0, w = chunk_parts(c)
                    if n == 0:
                        pool.wait_ge(d_copied, 2 * it + 2)
                    old = POOL_CHUNKS[(n - ZP_RING) % NPOOL]
                    wait(pool, g_ready, NACT * (it if n >= ZP_RING else it - 1) + ACT_INDEX[old] + 1)
                    dt_ = pair[par][:, DMG, half, LPAD + t0:LPAD + T]
                    o = zp[:, n % ZP_RING, 0:4 * w].rearrange("p (i t) -> p i t", i=4)
                    pool.tensor_tensor(o, shifted_rows(pair[par], DMG, half, pr, w),
                                       dt_.unsqueeze(1).to_broadcast([P, 4, w]), ALU.subtract).then_inc(zp_ready, 1)

                def inverse_deviation(b, var, stats, shifted_var, step_done, result, done):
                    pool.wait_ge(var, 4 * (b + 1))
                    pool.tensor_tensor(shifted_var[:, :], stats[:, :, 1], epst[:, :], ALU.add).then_inc(step_done, 1)
                    pool.wait_ge(step_done, b + 1)
                    pool.tensor_tensor(result[:, :], shifted_var[:, :], mhalf[:, :], ALU.pow).then_inc(done, 1)

                for k in range(NSLOT):
                    if exists(it, 0) and (DMG, k) in POOL_CHUNKS:
                        differences(POOL_CHUNKS.index((DMG, k)), k)
                    if at(k, it, POOL_AT["rstd1"]):
                        inverse_deviation(it - POOL_AT["rstd1"] // STEP, var_ready, mv, ve, rs_step, rstd, rstd_ready)
                    if at(k, it, POOL_AT["rstd2"]):
                        inverse_deviation(it - POOL_AT["rstd2"] // STEP, var2_ready, mv2, ve2, rs2_step, rstd2, rstd2_ready)

            iterations(pool, body)

        @block.vector
        def _(dve):
            step = [0]

            def mark(ins):
                step[0] += 1
                ins.then_inc(dve_const, 1)

            mark(dve.memset(logit[0][:, :], 0.0))
            assert step[0] == DVE_ZERO
            mark(dve.memset(ones[:, :, :], 0.0))
            mark(dve.memset(ctr[:, :, :, :], 0.0))
            for q in range(2):
                mark(dve.memset(pair[q][:, :, :, 0:LPAD], 0.0))
            dve.wait_ge(dve_const, step[0])
            for h in range(4):
                mark(dve.memset(ones[:, h, HS * h:HS * h + HS], 1.0))
            dve.wait_ge(setup_in, SETUP_DMAS * 16)
            mark(dve.tensor_copy(wposrep.rearrange("d (h o) -> d h o", h=HH),
                                 wposr.unsqueeze(1).to_broadcast([16, HH, BD])))
            mark(dve.tensor_scalar(bcol[:, :], boraw[:, :], 0.5, None, ALU.mult))
            assert step[0] == DVE_A
            dve.wait_ge(pe_const, 1)
            dve.tensor_copy(cols[:, :], LB[:, 0:35]).then_inc(dve_const, 1)
            dve.wait_ge(dve_const, DVE_A + 1)
            dve.wait_ge(pool_const, POOL_CONSTS)
            for f in range(2):
                dve.tensor_tensor(bdg[:, f, :].rearrange("p (h o) -> p h o", h=HH),
                                  m8[:, :].unsqueeze(2).to_broadcast([P, HH, BD]),
                                  cols[:, 3 + BD * f:3 + BD * f + BD].unsqueeze(1).to_broadcast([P, HH, BD]),
                                  ALU.mult).then_inc(dve_const, 1)
            for f in range(2):
                for v in range(4):
                    dve.tensor_scalar(ctr[:, f, v, 8 * v:8 * v + 8], m8[:, :], cols[:, f:f + 1], None,
                                      ALU.mult).then_inc(dve_const, 1)
            dve.wait_ge(pe_const, 2)
            dve.tensor_copy(relR[:, :], LB[:, 64:64 + LAGS]).then_inc(dve_const, 1)
            dve.wait_ge(pe_const, 3)
            dve.tensor_copy(wpair[:, :, :], LD[:, :]).then_inc(dve_const, 1)
            dve.wait_ge(dve_const, DVE_ALL)

            def body(it, par):
                def ready(b, name):
                    dve.wait_ge(w_ready[BANK[name]], bank_use(b, name, COUNTED_BY_BLOCKS) + 1)

                def differences(kind, c):
                    n = DVE_CHUNKS.index((kind, c))
                    g, half, pr, t0, w = chunk_parts(c)
                    if kind == DMG:
                        dve.wait_ge(d_copied, 2 * it + 2)
                    else:
                        dve.wait_ge(a_copied, 2 * it + 1 + half)
                    old = DVE_CHUNKS[(n - ZV_RING) % NDVE]
                    wait(dve, g_ready, NACT * (it if n >= ZV_RING else it - 1) + ACT_INDEX[old] + 1)
                    z = zv[:, n % ZV_RING, 0:4 * w].rearrange("p (i t) -> p i t", i=4)
                    if kind == DMG:
                        dve.tensor_tensor(z, shifted_rows(pair[par], DMG, half, pr, w),
                                          PD[:, t0:T].unsqueeze(1).to_broadcast([P, 4, w]),
                                          ALU.subtract).then_inc(zv_ready, 1)
                        return
                    rows = shifted_rows(pair[par], BOND, half, pr, w)
                    for i in range(4):
                        lag = 8 * g + 2 * (3 - i) + pr
                        ins = dve.scalar_tensor_tensor(out=z[:, i, :], in0=rows[:, i, :],
                                                       scalar=relR[:, 63 - lag:64 - lag], in1=PA[half][:, t0:T],
                                                       op0=ALU.add, op1=ALU.subtract)
                    ins.then_inc(zv_ready, 1)

                def copy_a(b, buf, half):
                    dve.wait_ge(proj_ready, 4 * b + half + 3)
                    dve.tensor_copy(pair[buf][:, BOND, half, LPAD:], PA[half][:, :]).then_inc(a_copied, 1)

                def combine(b, buf, g):
                    if isinstance(b, int) and b == 0 and g == 0:
                        dve.wait_ge(scratch_zero, 64)
                    if isinstance(b, int) and b == 1 and g == 0:
                        dve.wait_ge(later_zero, 3)
                    if g == 0:
                        wait(dve, shifted[0], 256 * (b - 1))
                        wait(dve, shifted[1], 256 * (b - 1))
                    dve.wait_ge(tanh_done, NG * b + g + 1)
                    dve.wait_ge(g_used, NACT * b + ACT_INDEX[(BOND, 4 * g + 3)] + 1)
                    dve.scalar_tensor_tensor(out=logit[buf][:, T * g + 8 * g:T * g + T], in0=th[:, 8 * g:T], scalar=-5.0,
                                             in1=LB[:, 8 * g:T], op0=ALU.mult, op1=ALU.add).then_inc(logit_done, 1)

                def logits(b_stage):
                    return logit[(par + b_stage) % 2][:, 0:NG * T].rearrange("p (g t) -> p g t", g=NG)

                def group_max(b, lv, a):
                    if a == 0:
                        dve.wait_ge(logit_done, NG * (b + 1))
                        for g in range(NG):
                            w = 8 * g + 8
                            dve.tensor_tensor(lv[:, g, 0:w], lv[:, g, 0:w], maskt[:, LAGS - w:LAGS], ALU.min)\
                               .then_inc(masked, 1)
                        dve.wait_ge(masked, NG * (b + 1))
                    dve.tensor_reduce(t1[:, P * a:P * a + P], lv[:, :, P * a:P * a + P].rearrange("p g t -> p t g"),
                                      AX.X, ALU.max).then_inc(gmax_ready, 1)

                def lag_max(b):
                    ready(b, "maxT")
                    m = W[BANK["maxT"]][:, :].rearrange("p (a u h) -> p a h u", a=TT, u=8)
                    dve.tensor_reduce(max2[:, :].rearrange("p (a h) -> p a h", a=TT), m, AX.X,
                                      ALU.max).then_inc(w_free[BANK["maxT"]], 1)

                def subtract_max(b, lv, a):
                    if a == 0:
                        ready(b, "maxB")
                    t = slice(P * a, P * a + P)
                    ins = dve.tensor_tensor(lv[:, :, t], lv[:, :, t],
                                            W[BANK["maxB"]][:, t].unsqueeze(1).to_broadcast([P, NG, P]), ALU.subtract)
                    if a == TT - 1:
                        ins.then_inc(w_free[BANK["maxB"]], 1)

                def evict(b, tt):
                    name = f"ev{tt}b"
                    ready(b, name)
                    wait(dve, z_written[(tt - 2) % TT], 16 * (b + 1 if tt >= 2 else b))
                    src = W[BANK[name]][:, :].rearrange("p (g u h) -> p g u h", g=4, u=8)
                    dst = ev[:, tt % 2, :, 32:64].rearrange("p h (g u) -> p g u h", g=4)
                    dve.tensor_copy(dst, src).then_inc(w_free[BANK[name]], 1)

                def normalise(b, i):
                    w = W[BANK[f"heads{i}"]]
                    dve.wait_ge(band_used, NB * b + 4 * i + 4)
                    dve.reciprocal(t2[:, 256 * i:256 * i + 256], w[:, 256:512]).then_inc(recip_done, 1)
                    dve.wait_ge(recip_done, 2 * b + i + 1)
                    dve.tensor_tensor(t2[:, 256 * i:256 * i + 256], w[:, 0:256], t2[:, 256 * i:256 * i + 256],
                                      ALU.mult).then_inc(w_free[BANK[f"heads{i}"]], 1)

                def residual(b):
                    ready(b, "cproj")
                    dve.wait_ge(xr_in, 16 * (b + 1))
                    r = res[:, :, :].rearrange("p a c -> p (a c)")
                    dve.tensor_tensor(r, W[BANK["cproj"]][:, :], r, ALU.add).then_inc(w_free[BANK["cproj"]], 1)
                    dve.wait_ge(w_free[BANK["cproj"]], bank_use(b, "cproj") + 1)
                    for a in range(TT):
                        dve.bn_stats(st[:, a, :], res[:, a, :]).then_inc(stat_done, 1)
                    dve.wait_ge(stat_done, 4 * (b + 1))
                    dve.tensor_copy(mark_[:, 0:1], st[:, 0, 0:1])
                    for a in range(TT):
                        dve.bn_aggr(mv[:, a, :], st[:, a, :]).then_inc(var_ready, 1)

                def first_norm(b):
                    dve.wait_ge(rstd_ready, b + 1)
                    for a in range(TT):
                        dve.tensor_scalar(y[:, a, :], res[:, a, :], mv[:, a, 0:1], rstd[:, a:a + 1], ALU.subtract,
                                          ALU.mult).then_inc(y_ready, 1)

                def gate(b, hb):
                    dve.wait_ge(tanh_gate, KB * b + hb + 1)
                    hrow = hid1[:, hb, :]
                    dve.scalar_tensor_tensor(out=hrow, in0=hrow, scalar=1.0, in1=W[BANK[f"gate{hb}"]][:, :], op0=ALU.add,
                                             op1=ALU.mult).then_inc(w_free[BANK[f"gate{hb}"]], 1)
                    dve.wait_ge(w_free[BANK[f"gate{hb}"]], bank_use(b, f"gate{hb}") + 1)
                    ready(b, f"up{hb}")
                    dve.scalar_tensor_tensor(out=hrow, in0=hrow, scalar=s12[:, hb:hb + 1], in1=W[BANK[f"up{hb}"]][:, :],
                                             op0=ALU.mult, op1=ALU.mult).then_inc(w_free[BANK[f"up{hb}"]], 1)

                def mlp_residual(b):
                    ready(b, "mlpout")
                    wait(dve, out_done, 16 * b)
                    src = W[BANK["mlpout"]][:, :].rearrange("p (a c) -> p a c", a=TT)
                    dve.tensor_tensor(res2[:, :, :], src, w3sb[:, :].unsqueeze(1).to_broadcast([P, TT, C]),
                                      ALU.mult).then_inc(w_free[BANK["mlpout"]], 1)
                    dve.wait_ge(w_free[BANK["mlpout"]], bank_use(b, "mlpout") + 1)
                    dve.tensor_tensor(res2[:, :, :], res2[:, :, :], y[:, :, :], ALU.add).then_inc(res2_ready, 1)
                    dve.wait_ge(res2_ready, b + 1)
                    for a in range(TT):
                        dve.bn_stats(st2[:, a, :], res2[:, a, :]).then_inc(stat2_done, 1)
                    dve.wait_ge(stat2_done, 4 * (b + 1))
                    dve.tensor_copy(mark_[:, 1:2], st2[:, 0, 0:1])
                    for a in range(TT):
                        dve.bn_aggr(mv2[:, a, :], st2[:, a, :]).then_inc(var2_ready, 1)

                def second_norm(b):
                    dve.wait_ge(rstd2_ready, b + 1)
                    for a in range(TT):
                        dve.tensor_scalar(res2[:, a, :], res2[:, a, :], mv2[:, a, 0:1], rstd2[:, a:a + 1], ALU.subtract,
                                          ALU.mult).then_inc(out_ready, 1)

                if isinstance(it, int) and it == 1:
                    dve.wait_ge(weights_in, 16 * WEIGHT_DMAS)
                    dve.tensor_scalar(s1h[:, :], s1[:, :], 0.5, None, ALU.mult).then_inc(scales_made, 1)
                    dve.wait_ge(scales_made, 1)
                    dve.tensor_tensor(s12[:, :], s1h[:, :], s2[:, :], ALU.mult).then_inc(scales_made, 1)
                    dve.wait_ge(scales_made, 2)
                for k in range(NSLOT):
                    for half in range(2):
                        if at(k, it, DVE_AT["copy_a"][half]):
                            stage = DVE_AT["copy_a"][half] // STEP
                            copy_a(it - stage, (par + stage) % 2, half)
                    if exists(it, 0) and k in DVE_DAMAGE:
                        differences(DMG, k)
                    if exists(it, 0) and k >= LAG_B:
                        differences(BOND, k - LAG_B)
                    for g in range(NG):
                        if at(k, it, DVE_AT["combine"][g]):
                            stage = DVE_AT["combine"][g] // STEP
                            combine(it - stage, (par + stage) % 2, g)
                    for a in range(TT):
                        if at(k, it, DVE_AT["group_max"][a]):
                            stage = DVE_AT["group_max"][a] // STEP
                            group_max(it - stage, logits(stage), a)
                    if at(k, it, DVE_AT["lag_max"]):
                        lag_max(it - DVE_AT["lag_max"] // STEP)
                    for a in range(TT):
                        if at(k, it, DVE_AT["subtract"][a]):
                            stage = DVE_AT["subtract"][a] // STEP
                            subtract_max(it - stage, logits(stage), a)
                    for i in range(2):
                        if at(k, it, DVE_AT["evict_b"][i]):
                            evict(it - DVE_AT["evict_b"][i] // STEP, 2 * i + 1)
                    for i in range(2):
                        if at(k, it, DVE_AT["normalise"][i]):
                            normalise(it - DVE_AT["normalise"][i] // STEP, i)
                    if at(k, it, DVE_AT["residual"]):
                        residual(it - DVE_AT["residual"] // STEP)
                    if at(k, it, DVE_AT["norm1"]):
                        first_norm(it - DVE_AT["norm1"] // STEP)
                    for hb in range(KB):
                        if at(k, it, DVE_AT["gate"][hb]):
                            gate(it - DVE_AT["gate"][hb] // STEP, hb)
                    if at(k, it, DVE_AT["mlp_residual"]):
                        mlp_residual(it - DVE_AT["mlp_residual"] // STEP)
                    if at(k, it, DVE_AT["norm2"]):
                        second_norm(it - DVE_AT["norm2"] // STEP)

            iterations(dve, body)

        @block.scalar
        def _(act):
            def copy_projection(b, buf, i):
                act.wait_ge(proj_ready, 4 * b + i + 1)
                act.activation(pair[buf][:, DMG, 1 - i, LPAD:], PD[:, :], ACT.Copy).then_inc(d_copied, 1)

            def body(it, par):
                def ready(b, name):
                    act.wait_ge(w_ready[BANK[name]], bank_use(b, name, COUNTED_BY_BLOCKS) + 1)

                def gelu(kind, c):
                    n = ACT_INDEX[(kind, c)]
                    g, half, pr, t0, w = chunk_parts(c)
                    wait(act, g_used, NACT * it + n - G_RING + 1)
                    if (kind, c) in DVE_CHUNKS:
                        m = DVE_CHUNKS.index((kind, c))
                        act.wait_ge(zv_ready, NDVE * it + m + 1)
                        z = zv[:, m % ZV_RING, 0:4 * w]
                    else:
                        m = POOL_CHUNKS.index((kind, c))
                        act.wait_ge(zp_ready, NPOOL * it + m + 1)
                        z = zp[:, m % ZP_RING, 0:4 * w]
                    bias = cols[:, 2:3] if kind == DMG else 0.0
                    act.activation(gl[:, n % G_RING, 0:4 * w], z, ACT.Gelu, bias=bias).then_inc(g_ready, 1)

                def damage_tanh(b, g):
                    act.wait_ge(g_used, NACT * b + ACT_INDEX[(DMG, 4 * g + 3)] + 1)
                    wait(act, logit_done, NG * b + g)
                    act.activation(th[:, 8 * g:T], LD[:, 8 * g:T], ACT.Tanh, bias=bcol[:, 0:1],
                                   scale=0.5).then_inc(tanh_done, 1)

                def copy_max(b):
                    ready(b, "maxTT")
                    act.activation(maxrow, W[BANK["maxTT"]][0:H, :], ACT.Copy).then_inc(w_free[BANK["maxTT"]], 1)

                def exponent(b, stage):
                    act.wait_ge(w_free[BANK["maxB"]], bank_use(b, "maxB") + 1)
                    v = logit[(par + stage) % 2][:, 0:NG * T]
                    act.activation(v, v, ACT.Exp).then_inc(exp_done, 1)

                def evict(b, tt, part):
                    name = f"ev{tt}{'ab'[part]}"
                    ready(b, name)
                    wait(act, z_written[(tt - 2) % TT], 16 * (b + 1 if tt >= 2 else b))
                    src = W[BANK[name]][:, :].rearrange("p (g u h) -> p g u h", g=4, u=8)
                    dst = ev[:, tt % 2, :, 32 * part:32 * part + 32].rearrange("p h (g u) -> p g u h", g=4)
                    act.activation(dst, src, ACT.Copy).then_inc(w_free[BANK[name]], 1)

                def values(b, j):
                    name = f"val{j}"
                    ready(b, name)
                    wait(act, band_used, NB * b + 4 * j)
                    base = vpad[:, 0, 0, 0, 0:8]
                    dst = bass.AP(vpad, base.offset, [list(base.ap[0]), [128, 16], [40, 4], [1, HS]])
                    src = W[BANK[name]][:, :].rearrange("p (q h e) -> p q h e", q=16, h=4)
                    act.activation(dst, src, ACT.Copy).then_inc(w_free[BANK[name]], 1)

                def y_transposed(b):
                    ready(b, "yT")
                    act.activation(yT, W[BANK["yT"]][:, :], ACT.Copy).then_inc(w_free[BANK["yT"]], 1)

                def gate_tanh(b, hb):
                    ready(b, f"gate{hb}")
                    act.activation(hid1[:, hb, :], W[BANK[f"gate{hb}"]][:, :], ACT.Tanh,
                                   scale=s1h[:, hb:hb + 1]).then_inc(tanh_gate, 1)

                def hidden(b, layer, ob):
                    name = f"h{layer}_{ob}"
                    ready(b, name)
                    dst, sc = ((hid2, sh1), (hid1, sh2))[layer - 1]
                    act.activation(dst[:, ob, :], W[BANK[name]][:, :], ACT.Gelu,
                                   scale=sc[:, ob:ob + 1]).then_inc(w_free[BANK[name]], 1)

                if isinstance(it, int) and it == 1:
                    act.wait_ge(later_zero, 2)
                    act.wait_ge(weights_in, 16 * WEIGHT_DMAS)
                    act.wait_ge(scales_made, 1)
                for k in range(NSLOT):
                    if exists(it, 0) and k < NCH:
                        gelu(DMG, k)
                    for g in range(NG):
                        if at(k, it, ACT_AT["tanh"][g]):
                            damage_tanh(it - ACT_AT["tanh"][g] // STEP, g)
                    if exists(it, 0) and k >= LAG_B:
                        gelu(BOND, k - LAG_B)
                    for i in range(2):
                        stage = ACT_AT["proj"][i] // STEP
                        if at(k, it, ACT_AT["proj"][i]) and not (isinstance(it, int) and it == stage):
                            copy_projection(it - stage, (par + stage) % 2, i)
                    if at(k, it, ACT_AT["copy_max"]):
                        copy_max(it - ACT_AT["copy_max"] // STEP)
                    if at(k, it, ACT_AT["exp"]):
                        exponent(it - ACT_AT["exp"] // STEP, ACT_AT["exp"] // STEP)
                    for tt in range(TT):
                        if at(k, it, ACT_AT["evict_a"][tt]):
                            evict(it - ACT_AT["evict_a"][tt] // STEP, tt, 0)
                        if tt % 2 == 0 and at(k, it, ACT_AT["evict_b"][tt // 2]):
                            evict(it - ACT_AT["evict_b"][tt // 2] // STEP, tt, 1)
                    for j in range(2):
                        if at(k, it, ACT_AT["values"][j]):
                            values(it - ACT_AT["values"][j] // STEP, j)
                    if at(k, it, ACT_AT["yT"]):
                        y_transposed(it - ACT_AT["yT"] // STEP)
                    for hb in range(KB):
                        if at(k, it, ACT_AT["gate"][hb]):
                            gate_tanh(it - ACT_AT["gate"][hb] // STEP, hb)
                        if at(k, it, ACT_AT["h1"][hb]):
                            hidden(it - ACT_AT["h1"][hb] // STEP, 1, hb)
                        if at(k, it, ACT_AT["h2"][hb]):
                            hidden(it - ACT_AT["h2"][hb] // STEP, 2, hb)

            act.wait_ge(pool_const, POOL_CONSTS)
            act.activation(gl[:, 3, 0:1], maskt[:, 0:1], ACT.Gelu, bias=0.0)
            act.wait_ge(dve_const, DVE_ALL)
            for i in range(2):
                copy_projection(0, 0, i)
            iterations(act, body)

        @block.tensor
        def _(pe):
            def project(b, i):
                kind, half, bank = ((DMG, 1, PD), (DMG, 0, PD), (BOND, 0, PA[0]), (BOND, 1, PA[1]))[i]
                if i == 1:
                    pe.wait_ge(d_copied, 2 * b + 1)
                elif not (isinstance(b, int) and b == 0):
                    if i == 0:
                        pe.wait_ge(xp_in, 16 * b)
                    last = {0: (DMG, DVE_DAMAGE[-1]), 2: (BOND, NCH - 3), 3: (BOND, NCH - 1)}[i]
                    pe.wait_ge(zv_ready, NDVE * (b - 1) + DVE_CHUNKS.index(last) + 1)
                pe.matmul(bank[:, :], wpair[:, 2 * kind + half, :], xTp[:, :], start=True,
                          stop=True).then_inc(proj_ready, 1)

            pe.wait_ge(setup_in, SETUP_DMAS * 16)
            pe.wait_ge(pool_const, POOL_CONSTS)
            pe.wait_ge(dve_const, DVE_A)
            pe.matmul(LB[:, 0:35], rep, wvec, start=True, stop=True).then_inc(pe_const, 1)
            pe.wait_ge(dve_const, DVE_A + 1)
            pe.matmul(LB[:, 64:64 + LAGS], wposrep, relt, start=True, stop=True).then_inc(pe_const, 1)
            pe.wait_ge(dve_const, DVE_A + 3)
            for f in range(2):
                for half in range(2):
                    mm = pe.matmul(LD[:, P * (2 * f + half):P * (2 * f + half) + P], wdt[:, half, :], bdg[:, f, :],
                                   start=True, stop=True)
            mm.then_inc(pe_const, 1)
            pe.wait_ge(dve_const, DVE_ALL)
            for i in range(4):
                project(0, i)

            def body(it, par):
                def free(b, name):
                    wait(pe, w_free[BANK[name]], bank_use(b, name))
                    return W[BANK[name]]

                def done(name, mm):
                    mm.then_inc(w_ready[BANK[name]], 1)

                def contract(kind, c):
                    n = ACT_INDEX[(kind, c)]
                    g, half, pr, t0, w = chunk_parts(c)
                    bank = (LB, LD)[kind]
                    if c % 4 == 0:
                        wait(pe, (logit_done, tanh_done)[kind], NG * it + g)
                    pe.wait_ge(g_ready, NACT * it + n + 1)
                    gv = gl[:, n % G_RING, 0:4 * w].rearrange("p (i t) -> p i t", i=4)
                    for q in range(4):
                        mm = pe.matmul(bank[32 * q:32 * q + 32, t0:T], ctr[:, kind, 2 * pr + half, :], gv[:, 3 - q, :],
                                       start=(c % 4 == 0), stop=(c % 4 == 3))
                    mm.then_inc(g_used, 1)

                def max_transposed(b):
                    pe.wait_ge(gmax_ready, TT * (b + 1))
                    w = free(b, "maxT")
                    for a in range(TT):
                        mm = pe.transpose(w[:, P * a:P * a + P], t1[:, P * a:P * a + P], ident[:, :])
                    done("maxT", mm)

                def max_rows(b):
                    pe.wait_ge(w_free[BANK["maxT"]], bank_use(b, "maxT") + 1)
                    w = free(b, "maxTT")
                    for a in range(TT):
                        mm = pe.transpose(w[0:H, P * a:P * a + P], max2[:, H * a:H * a + H], ident[:, :])
                    done("maxTT", mm)

                def max_broadcast(b):
                    pe.wait_ge(w_free[BANK["maxTT"]], bank_use(b, "maxTT") + 1)
                    w = free(b, "maxB")
                    done("maxB", pe.matmul(w[:, :], selm[:, :], maxrow, start=True, stop=True))

                def weights_transposed(b, tt, i):
                    pe.wait_ge(shifted[tt % 2], 256 * b + 128 * (tt // 2) + 128)
                    name = f"ev{tt}{'ab'[i]}"
                    w = free(b, name)
                    for g in range(4):
                        mm = pe.transpose(w[:, P * g:P * g + P], esh[:, tt % 2, 4 * i + g, :], ident[:, :])
                    done(name, mm)

                def value_rows(b, j):
                    name = f"val{j}"
                    pe.wait_ge(xv_in, 16 * (b + 1))
                    w = free(b, name)
                    for i in range(4):
                        s0 = 64 * (4 * j + i) + 1
                        mm = pe.matmul(w[:, P * i:P * i + P], xTv[:, s0:s0 + P], wval[:, :], start=True, stop=True)
                    done(name, mm)

                def banded(b, k):
                    if k % 4 == 0:
                        free(b, f"heads{k // 4}")
                        pe.wait_ge(w_free[BANK[f"val{k // 4}"]], bank_use(b, f"val{k // 4}") + 1)
                    pe.wait_ge(band_in[k % 2], 64 * b + 16 * (k // 2) + 16)
                    w = W[BANK[f"heads{k // 4}"]]
                    for wt, c0 in ((vpad[:, k % 4, :, :, :], 0), (None, 256)):
                        t = slice(c0 + 64 * (k % 4), c0 + 64 * (k % 4) + 64)
                        for h in range(4):
                            for q in range(4):
                                lhs = ones[:, h, :] if wt is None else wt[:, q, h, :]
                                mm = pe.matmul(w[32 * q:32 * q + 32, t], lhs, band[:, k % 2, 4 * q + h, :],
                                               start=(h == 0), stop=(h == 3))
                    mm.then_inc(band_used, 1)

                def output_projection(b):
                    pe.wait_ge(w_free[BANK["heads1"]], bank_use(b, "heads1") + 1)
                    w = free(b, "cproj")
                    for a in range(TT):
                        mm = pe.matmul(w[:, P * a:P * a + P], t2[:, P * a:P * a + P], wcp[:, :], start=True, stop=True)
                    done("cproj", mm)

                def y_transposed(b):
                    pe.wait_ge(y_ready, 4 * (b + 1))
                    w = free(b, "yT")
                    for a in range(TT):
                        mm = pe.transpose(w[:, P * a:P * a + P], y[:, a, :], ident[:, :])
                    done("yT", mm)

                def gate_up(b, hb):
                    if hb == 0:
                        pe.wait_ge(w_free[BANK["yT"]], bank_use(b, "yT") + 1)
                    for name, wt in ((f"gate{hb}", w1t), (f"up{hb}", w2t)):
                        w = free(b, name)
                        done(name, pe.matmul(w[:, :], wt[:, P * hb:P * hb + P], yT[:, :], start=True, stop=True))

                def hidden(b, layer, ob, part):
                    name = f"h{layer}_{ob}"
                    src, wt = ((hid1, h1t), (hid2, h2t))[layer - 1]
                    if part == 0:
                        free(b, name)
                        if ob == 0:
                            last = ("up3", "h1_3")[layer - 1]
                            pe.wait_ge(w_free[BANK[last]], bank_use(b, last) + 1)
                    w = W[BANK[name]]
                    for kb in range(2 * part, 2 * part + 2):
                        mm = pe.matmul(w[:, :], wt[:, kb, P * ob:P * ob + P], src[:, kb, :], start=(kb == 0),
                                       stop=(kb == KB - 1))
                    if part == 1:
                        done(name, mm)

                def mlp_out(b, part):
                    if part == 0:
                        free(b, "mlpout")
                        pe.wait_ge(w_free[BANK["h2_3"]], bank_use(b, "h2_3") + 1)
                    w = W[BANK["mlpout"]]
                    for a in range(2 * part, 2 * part + 2):
                        for kb in range(KB):
                            mm = pe.matmul(w[:, P * a:P * a + P], hid1[:, kb, P * a:P * a + P], w3t[:, kb, :],
                                           start=(kb == 0), stop=(kb == KB - 1))
                    if part == 1:
                        done("mlpout", mm)

                def mlp_item(b, name, part):
                    if name == "mlpout":
                        mlp_out(b, part)
                    else:
                        hidden(b, int(name[1]), int(name[3]), part)

                if isinstance(it, int) and it == 1:
                    pe.wait_ge(weights_in, 16 * WEIGHT_DMAS)
                for k in range(NSLOT):
                    if exists(it, 0) and k < NCH:
                        contract(DMG, k)
                    if at(k, it, PE_MLP["yT"]):
                        y_transposed(it - PE_STAGE["yT"])
                    for hb in range(KB):
                        if at(k, it, PE_MLP[f"gate{hb}"]):
                            gate_up(it - PE_STAGE[f"gate{hb}"], hb)
                    for name in PE_MLP_SECOND:
                        if at(k, it, PE_MLP[name]):
                            mlp_item(it - PE_STAGE[name], name, 0)
                        if at(k, it, PE_MLP_SECOND[name]):
                            mlp_item(it - PE_MLP_SECOND[name] // STEP, name, 1)
                    if exists(it, 0) and k >= LAG_B:
                        contract(BOND, k - LAG_B)
                    if at(k, it, PE_ATT["cproj"]):
                        output_projection(it - PE_STAGE["cproj"])
                    if at(k, it, PE_ATT["maxT"]):
                        max_transposed(it - PE_STAGE["maxT"])
                    if at(k, it, PE_ATT["maxTT"]):
                        max_rows(it - PE_STAGE["maxTT"])
                    if at(k, it, PE_ATT["maxB"]):
                        max_broadcast(it - PE_STAGE["maxB"])
                    if at(k, it, PE_ATT["val0"]):
                        value_rows(it - PE_STAGE["val0"], 0)
                    for tt in range(TT):
                        for i in range(2):
                            name = f"ev{tt}{'ab'[i]}"
                            if at(k, it, PE_ATT[name]):
                                weights_transposed(it - PE_STAGE[name], tt, i)
                    if at(k, it, PE_ATT["val1"]):
                        value_rows(it - PE_STAGE["val1"], 1)
                    for n in range(NB):
                        if at(k, it, PE_BLOCK[n]):
                            banded(it - PE_BLOCK[n] // STEP, n)
                    for i in range(4):
                        stage = PE_PROJ[i] // STEP
                        if at(k, it, PE_PROJ[i]) and not (isinstance(it, int) and it == stage):
                            project(it - stage, i)

            iterations(pe, body)


SETUP_DMAS = 10
WEIGHT_DMAS = 12
POOL_CONSTS = 13
DVE_ZERO = 1
DVE_A = 11
DVE_ALL = DVE_A + 1 + 2 + 8 + 2


_INS = ["xT", "x", "W_dispT", "W_val", "relT", "W_strain", "W_pos", "W_bond", "W_dmg", "b_dmg", "W_dmg_out",
        "b_dmg_out", "W_cproj", "w1T", "w1_s", "w2T", "w2_s", "h1T", "h1_s", "h2T", "h2_s", "w3T", "w3_s"]


def kernel(**inputs):
    import numpy as np
    import concourse.bacc as bacc
    from concourse.bass_utils import run_bass_kernel_spmd

    a = {k: np.asarray(v) for k, v in inputs.items()}
    x = a["L0_attn_x"]
    given = {
        "xT": x.transpose(2, 0, 1).reshape(x.shape[2], -1), "x": x,
        "W_dispT": a["L0_attn_W_disp"].T, "relT": a["L0_attn_rel_pos_emb"].T,
        **{n: a[f"L0_attn_{n}"] for n in ("W_val", "W_strain", "W_pos", "W_bond", "W_dmg", "b_dmg", "W_dmg_out",
                                          "b_dmg_out", "W_cproj")},
        **{f"{n}T": a[f"L0_ffn_{n}_w"].T for n in ("w1", "w2", "h1", "h2", "w3")},
        **{f"{n}_s": a[f"L0_ffn_{n}_s"].reshape(-1, P).T for n in ("w1", "w2", "h1", "h2")},
        "w3_s": a["L0_ffn_w3_s"],
    }
    nc = bacc.Bacc("TRN2", target_bir_lowering=False, num_devices=1)
    arrays, args = {}, []
    for name in _INS:
        v = np.ascontiguousarray(given[name])
        arrays[f"in_{name}"] = v
        args.append(nc.dram_tensor(f"in_{name}", v.shape, mybir.dt.from_np(v.dtype), kind="ExternalInput").ap())
    args.append(nc.dram_tensor("out_0", x.shape, F32, kind="ExternalOutput").ap())
    block_kernel(nc, *args)
    r = run_bass_kernel_spmd(nc, [arrays], core_ids=[0])
    return r.results[0]["out_0"]
```
